# Optimizing a Trainium2 kernel written in Bass

```python
import numpy as np
import jax
import jax.numpy as jnp

def _softmax(x, axis=-1):
    return jax.nn.softmax(x, axis=axis)

def _gelu(x):
    return jax.nn.gelu(x, approximate=True)

def _silu(x):
    return jax.nn.silu(x)

def _sigmoid(x):
    return jax.nn.sigmoid(x)

def _layernorm(x, axis=-1, eps=1e-05):
    m = jnp.mean(x, axis=axis, keepdims=True)
    v = jnp.var(x, axis=axis, keepdims=True)
    return (x - m) / jnp.sqrt(v + eps)

def _scatter_add(tgt, idx, src, axis=0):
    return tgt.at[idx].add(src)

def _segment_sum(src, seg, n):
    return jax.ops.segment_sum(src, seg, n)
kernel_name = 'mk_prb_d1_jaxref_r8_6c077e'

def setup_inputs(seed: int=0):
    np.random.seed(seed)
    _w = jnp.asarray

    def _L0_attn_setup():
        import jax, jax.numpy as jnp
        import numpy as np
        DMODEL = 128
        Q_HEADS = 16
        KV_HEADS = 4
        DHEAD = 64
        SEQ = 256
        TOP_K = 64
        ROPE_BASE = 10000.0
        NEG_INF = -1e+30

        def rope_cos_sin(seq_len, dhead, base):
            inv_freq = 1.0 / base ** (jnp.arange(0, dhead, 2, dtype=jnp.float32) / dhead)
            t = jnp.arange(seq_len, dtype=jnp.float32)
            angles = jnp.outer(t, inv_freq)
            emb = jnp.concatenate([angles, angles], axis=-1)
            return (jnp.cos(emb), jnp.sin(emb))

        def rotate_half(x):
            x1, x2 = jnp.split(x, 2, axis=-1)
            return jnp.concatenate([-x2, x1], axis=-1)

        def apply_rope(x, cos, sin):
            return x * cos[None, None] + rotate_half(x) * sin[None, None]
        key = jax.random.key(seed)
        ks = jax.random.split(key, 5)
        s = 0.02
        return {'x': jax.random.normal(ks[0], (1, SEQ, DMODEL), jnp.float32), 'Wq': jax.random.normal(ks[1], (Q_HEADS * DHEAD, DMODEL), jnp.float32) * s, 'Wk': jax.random.normal(ks[2], (KV_HEADS * DHEAD, DMODEL), jnp.float32) * s, 'Wv': jax.random.normal(ks[3], (KV_HEADS * DHEAD, DMODEL), jnp.float32) * s, 'Wo': jax.random.normal(ks[4], (DMODEL, Q_HEADS * DHEAD), jnp.float32) * s}
    _L0_attn_in = _L0_attn_setup()

    def _L0_ffn_setup():
        import jax, jax.numpy as jnp
        import numpy as np
        DIM = 128

        def _reference_tuple_inner(x, W_r, W_k, W_v, mu_r, mu_k):
            B, T, C = x.shape
            x_prev = jnp.concatenate([jnp.zeros((B, 1, C), x.dtype), x[:, :-1, :]], axis=1)
            xr = mu_r * x + (1.0 - mu_r) * x_prev
            xk = mu_k * x + (1.0 - mu_k) * x_prev
            r = jax.nn.sigmoid(jnp.einsum('btc,dc->btd', xr, W_r))
            k = jnp.einsum('btc,dc->btd', xk, W_k)
            k_act = jnp.square(jax.nn.relu(k))
            out = r * jnp.einsum('btc,dc->btd', k_act, W_v)
            new_state = x[:, -1, :]
            return (out, new_state)
        key = jax.random.key(seed)
        ks = jax.random.split(key, 6)
        B, T, C = (8, 256, DIM)
        x = jax.random.normal(ks[0], (B, T, C), dtype=jnp.float32)
        s = 1.0 / np.sqrt(C)
        W_r = jax.random.uniform(ks[1], (C, C), jnp.float32, -s, s)
        W_k = jax.random.uniform(ks[2], (C, C), jnp.float32, -s, s)
        W_v = jax.random.uniform(ks[3], (C, C), jnp.float32, -s, s)
        mu_r = jax.random.uniform(ks[4], (C,), jnp.float32)
        mu_k = jax.random.uniform(ks[5], (C,), jnp.float32)
        return {'x': x, 'W_r': W_r, 'W_k': W_k, 'W_v': W_v, 'mu_r': mu_r, 'mu_k': mu_k}
    _L0_ffn_in = _L0_ffn_setup()
    _d = {'L0_attn_x': _L0_attn_in['x'], 'L0_attn_Wq': _L0_attn_in['Wq'], 'L0_attn_Wk': _L0_attn_in['Wk'], 'L0_attn_Wv': _L0_attn_in['Wv'], 'L0_attn_Wo': _L0_attn_in['Wo'], 'L0_ffn_W_r': _L0_ffn_in['W_r'], 'L0_ffn_W_k': _L0_ffn_in['W_k'], 'L0_ffn_W_v': _L0_ffn_in['W_v'], 'L0_ffn_mu_r': _L0_ffn_in['mu_r'], 'L0_ffn_mu_k': _L0_ffn_in['mu_k']}
    _x0 = _d['L0_attn_x']
    _d['L0_attn_x'] = jax.random.normal(jax.random.fold_in(jax.random.key(seed), 1), (2, 1024, 128), dtype=_x0.dtype)
    del _x0
    return _d

def reference(L0_attn_x, L0_attn_Wq, L0_attn_Wk, L0_attn_Wv, L0_attn_Wo, L0_ffn_W_r, L0_ffn_W_k, L0_ffn_W_v, L0_ffn_mu_r, L0_ffn_mu_k):

    def _L0_attn_ref(x, Wq, Wk, Wv, Wo):
        import jax, jax.numpy as jnp
        import numpy as np
        DMODEL = 128
        Q_HEADS = 16
        KV_HEADS = 4
        DHEAD = 64
        SEQ = 256
        TOP_K = 64
        ROPE_BASE = 10000.0
        NEG_INF = -1e+30

        def rope_cos_sin(seq_len, dhead, base):
            inv_freq = 1.0 / base ** (jnp.arange(0, dhead, 2, dtype=jnp.float32) / dhead)
            t = jnp.arange(seq_len, dtype=jnp.float32)
            angles = jnp.outer(t, inv_freq)
            emb = jnp.concatenate([angles, angles], axis=-1)
            return (jnp.cos(emb), jnp.sin(emb))

        def rotate_half(x):
            x1, x2 = jnp.split(x, 2, axis=-1)
            return jnp.concatenate([-x2, x1], axis=-1)

        def apply_rope(x, cos, sin):
            return x * cos[None, None] + rotate_half(x) * sin[None, None]
        B, S, _ = x.shape
        cos, sin = rope_cos_sin(S, DHEAD, ROPE_BASE)
        q = (x @ Wq.T).reshape(B, S, Q_HEADS, DHEAD).transpose(0, 2, 1, 3)
        k = (x @ Wk.T).reshape(B, S, KV_HEADS, DHEAD).transpose(0, 2, 1, 3)
        v = (x @ Wv.T).reshape(B, S, KV_HEADS, DHEAD).transpose(0, 2, 1, 3)
        q = apply_rope(q, cos, sin)
        k = apply_rope(k, cos, sin)
        groups = Q_HEADS // KV_HEADS
        k = jnp.repeat(k, groups, axis=1)
        v = jnp.repeat(v, groups, axis=1)
        scores = jnp.einsum('bhqd,bhkd->bhqk', q, k) / np.sqrt(DHEAD)
        causal_mask = jnp.triu(jnp.ones((S, S), bool), k=1)
        scores = jnp.where(causal_mask[None, None], NEG_INF, scores)
        topk_vals, _ = jax.lax.top_k(scores, TOP_K)
        threshold = topk_vals[..., -1:]
        scores = jnp.where(scores < threshold, NEG_INF, scores)
        weights = jax.nn.softmax(scores, axis=-1)
        out = jnp.einsum('bhqk,bhkd->bhqd', weights, v)
        out = out.transpose(0, 2, 1, 3).reshape(B, S, Q_HEADS * DHEAD)
        return out @ Wo.T

    def _L0_ffn_ref(x, W_r, W_k, W_v, mu_r, mu_k):
        import jax, jax.numpy as jnp
        import numpy as np
        DIM = 128

        def _reference_tuple_inner(x, W_r, W_k, W_v, mu_r, mu_k):
            B, T, C = x.shape
            x_prev = jnp.concatenate([jnp.zeros((B, 1, C), x.dtype), x[:, :-1, :]], axis=1)
            xr = mu_r * x + (1.0 - mu_r) * x_prev
            xk = mu_k * x + (1.0 - mu_k) * x_prev
            r = jax.nn.sigmoid(jnp.einsum('btc,dc->btd', xr, W_r))
            k = jnp.einsum('btc,dc->btd', xk, W_k)
            k_act = jnp.square(jax.nn.relu(k))
            out = r * jnp.einsum('btc,dc->btd', k_act, W_v)
            new_state = x[:, -1, :]
            return (out, new_state)
        return _reference_tuple_inner(x, W_r, W_k, W_v, mu_r, mu_k)[0]
    x = L0_attn_x
    xn = _layernorm(x, axis=-1)
    x = x + _L0_attn_ref(xn, L0_attn_Wq, L0_attn_Wk, L0_attn_Wv, L0_attn_Wo) + _L0_ffn_ref(xn, L0_ffn_W_r, L0_ffn_W_k, L0_ffn_W_v, L0_ffn_mu_r, L0_ffn_mu_k)
    return x

_drawn_inputs = setup_inputs


def setup_inputs(seed=0):
    import zlib

    import numpy as np

    out = dict(_drawn_inputs(seed))
    spreads = {}
    factors = {'L0_attn_Wq': 7.636, 'L0_attn_Wk': 7.719, 'L0_ffn_W_r': 3.137, 'L0_ffn_mu_r': 6.185}
    for name, (base, spread) in spreads.items():
        noise = np.random.default_rng([zlib.crc32(name.encode()), seed]).standard_normal(out[name].shape)
        drawn = base * np.exp(spread * noise) if base else spread * noise
        out[name] = jnp.asarray(drawn.astype(out[name].dtype))
    for name, factor in factors.items():
        out[name] = (out[name] * factor).astype(out[name].dtype)
    return out
```

```python
import math
from contextlib import ExitStack

import numpy as np
import concourse.bass as bass
from concourse import mybir

F32 = mybir.dt.float32
BF16 = mybir.dt.bfloat16
I32 = mybir.dt.int32
ALU = mybir.AluOpType
ACT = mybir.ActivationFunctionType
AXIS = mybir.AxisListType

B, S, D = 2, 1024, 128
HEADS, KV, DH = 16, 4, 64
GROUP = HEADS // KV
PAIRS = HEADS // 2
P = 128
TILES = S // P
TOPK = 64
NEG = -1e30
EPS = 1e-5
BANK = 512

AIM_FIRST, AIM = 69.0, 72.0
WINDOW = 24
SEGMENTS = 8
BIG = 3e38

C_IDENT, C_MASK, C_RANK = 0, 128, 256
C_Z, C_STEP, C_AIM = 288, 296, 304
C_OPEN, C_SEARCHED = 312, 313
C_WIDTH = 320
R_COSQ, R_SINQ, R_COSK, R_SINK = 0, 512, 1024, 1536

ORDER = list(range(TILES - 1, -1, -1))
GROUPS = [(t, kv) for t in ORDER for kv in range(KV)]
NG = len(GROUPS)
RING = 3
PTS = 3
DRING = 3


def density(z):
    return math.exp(-z * z / 2) / math.sqrt(2 * math.pi)


def deviate(share):
    low, high = -8.0, 8.0
    for _ in range(60):
        z = (low + high) / 2
        low, high = (z, high) if 0.5 * math.erfc(z / math.sqrt(2)) > share else (low, z)
    return low


def constant_tables():
    rotary = np.zeros((P, 4 * 512), np.float32)
    inv = (1.0 / np.float32(10000.0) ** (np.arange(0, DH, 2, dtype=np.float32) / DH)).astype(np.float32)
    angle = np.outer(np.arange(S, dtype=np.float32), inv).astype(np.float32)
    cos = np.concatenate([np.cos(angle), np.cos(angle)], -1)
    sin = np.concatenate([-np.sin(angle), np.sin(angle)], -1)

    def rows(a):
        return a.reshape(TILES, P, DH).transpose(1, 0, 2).reshape(P, TILES * DH)
    scale = DH ** -0.5
    rotary[:, R_COSQ:R_COSQ + 512] = rows(cos) * scale
    rotary[:, R_SINQ:R_SINQ + 512] = rows(sin) * scale
    rotary[:, R_COSK:R_COSK + 512] = rows(cos)
    rotary[:, R_SINK:R_SINK + 512] = rows(sin)
    table = np.zeros((P, C_WIDTH), np.float32)
    table[:, C_IDENT:C_IDENT + P] = np.eye(P)
    table[:, C_MASK:C_MASK + P] = np.triu(np.full((P, P), NEG), 1)
    table[:, C_RANK:C_RANK + WINDOW] = np.arange(WINDOW)
    for t in range(TILES):
        for p in range(P):
            valid = t * P + p + 1
            if valid <= TOPK:
                continue
            z = deviate(min(AIM_FIRST / valid, 0.97))
            table[p, C_Z + t] = z
            table[p, C_STEP + t] = 1.0 / (valid * density(z))
            table[p, C_AIM + t] = min(AIM, (valid + TOPK) / 2) - (t + 1) * P / 2
    table[:TOPK, C_OPEN] = BIG
    table[TOPK:, C_SEARCHED] = 1.0
    return table, rotary


def build(nc, x, wqT, wkT, wvT, woT, wrT, wkfT, wvfT, mu_r, mu_k, table, rotary, out):
    ctx = ExitStack()
    with ctx:
        def sb(name, shape, dt=F32):
            return ctx.enter_context(nc.sbuf_tensor(name, shape, dt))

        def sem(name):
            return ctx.enter_context(nc.semaphore(name))

        consts = sb("consts", [P, C_WIDTH])
        ident = consts[:, C_IDENT:C_IDENT + P]
        ident16 = sb("ident16", [P, P], BF16)
        mask16 = sb("mask16", [P, P], BF16)
        ones = sb("ones", [P, 1])
        eps = sb("eps", [P, 1])
        Wo = sb("Wo", [P, PAIRS, D])
        mix = sb("mix", [P, 4])

        QT = sb("QT", [P, PAIRS, S])
        KT = sb("KT", [P, KV, 2, S])
        V = sb("V", [P, TILES, KV, DH + 1])
        resid = sb("resid", [P, TILES, D])
        base = sb("base", [P, TILES, HEADS])
        slope = sb("slope", [P, TILES, HEADS])

        depth = sb("depth", [P, DRING, GROUP, S])
        weight = sb("weight", [P, RING, GROUP, S])
        Wq = weight[:, 1, 3, :]
        Wk = weight[:, 0, 1, 0:256]
        Wv = weight[:, 0, 1, 256:512]
        Wr = weight[:, 0, 1, 512:640]
        Wkf = weight[:, 0, 1, 640:768]
        Wvf = weight[:, 0, 1, 768:896]
        rot = [depth[:, 1, 1, 0:512], depth[:, 1, 1, 512:1024], depth[:, 1, 3, 0:512], depth[:, 1, 3, 512:1024]]
        xin = depth[:, 0, 0, :].rearrange("p (t c) -> p t c", t=TILES)
        xn = depth[:, 0, 1, :].rearrange("p (t c) -> p t c", t=TILES)
        xnT = depth[:, 0, 2, :]
        qcos = depth[:, 1, 0:1, :]
        qsin = depth[:, 1, 2:3, :]
        qrow = weight[:, 0, 0:1, :]
        prod = depth[:, 0, 3, :]
        kcos = weight[:, 0, 2, 0:256]
        ksin = weight[:, 0, 2, 256:512]
        krow = weight[:, 0, 3, 0:768].rearrange("p (k c) -> p k c", k=KV)
        gram = weight[:, 1, 0, 0:520].rearrange("p (k c) -> p k c", k=KV)
        ssum = weight[:, 1, 1, 0:128].rearrange("p (t h) -> p t h", t=TILES)
        ssq = weight[:, 1, 1, 128:256].rearrange("p (t h) -> p t h", t=TILES)
        mean = weight[:, 1, 1, 256:384].rearrange("p (t h) -> p t h", t=TILES)
        var = weight[:, 1, 1, 384:512].rearrange("p (t h) -> p t h", t=TILES)
        dev = weight[:, 1, 1, 512:640].rearrange("p (t h) -> p t h", t=TILES)
        bn = weight[:, 1, 2, 0:48].rearrange("p (t c) -> p t c", t=TILES)
        mv = weight[:, 1, 2, 48:64].rearrange("p (t c) -> p t c", t=TILES)
        rstd = weight[:, 1, 2, 64:72]
        std = weight[:, 1, 2, 72:80]
        prevT = weight[:, 2, 0, :]
        xrT = weight[:, 2, 1, :]
        xkT = weight[:, 2, 2, :]
        relu = weight[:, 2, 3, :]
        kact = depth[:, 1, 0, :]
        gate = depth[:, 1, 2, :]
        gden = depth[:, 0, 3, :]

        zbuf = sb("zbuf", [P, 2, S])
        junk = sb("junk", [P, 2, S], BF16)
        PT = sb("PT", [P, PTS, BANK])
        heads_out = sb("heads_out", [P, HEADS * DH])
        yout = sb("yout", [P, D])
        attn_out = sb("attn_out", [P, D])
        SR = 4
        rowmax = sb("rowmax", [P, SR, GROUP])
        tau1 = sb("tau1", [P, SR, GROUP])
        tau2 = sb("tau2", [P, SR, GROUP])
        tau3 = sb("tau3", [P, SR, GROUP])
        sign1 = sb("sign1", [P, SR, GROUP])
        sign2 = sb("sign2", [P, SR, GROUP])
        sign3 = sb("sign3", [P, SR, GROUP])
        step_a = sb("step_a", [P, GROUP])
        step_b = sb("step_b", [P, GROUP])
        step_c = sb("step_c", [P, GROUP])
        step_d = sb("step_d", [P, GROUP])
        rank = sb("rank", [P, SR, GROUP])
        outside = sb("outside", [P, SR, GROUP])
        cand = sb("cand", [P, GROUP, SEGMENTS, 8])
        rest = sb("rest", [P, GROUP, SEGMENTS * 8])
        sorted24 = sb("sorted24", [P, GROUP, WINDOW])
        pick = sb("pick", [P, GROUP, WINDOW])
        segmin = sb("segmin", [P, GROUP])
        fail = sb("fail", [P, GROUP + 1])
        fail_b = sb("fail_b", [P, GROUP])
        fail_c = sb("fail_c", [P, GROUP])
        failed = sb("failed", [1, GROUP + 1], I32)
        thr = sb("thr", [P, 2, GROUP])
        best8 = sb("best8", [P, 8])
        outT = sb("outT", [DH + 1, BANK])
        rden = sb("rden", [P, GROUP])
        slow = zbuf[:, 0, :]

        psum = ctx.enter_context(nc.psum_tensor("psum", [P, 8, BANK], F32))

        names = """tables_loaded x_loaded p_stat p_std p_rstd p_xn p_xnT p_xnT_read p_proj p_proj_read p_rope p_kvcopied
            p_qT p_qT_read p_kT p_kT_read p_gram p_gram_read p_stats p_stats_read p_var p_dev p_pad p_mixed p_ffn
            p_relu p_exp p_kact p_v dve_step pool_step act_step thr_step
            scores_done scores_read depth_ready exp_ready tau1_ready tau2_ready tau3_ready count1 count2 count3
            fail_ready fail_summed fail_read weight_ready chunk_done chunk_read chunk_used sums_read back_done out_read
            attn_ready y_read stored slow_step rank_ready""".split()
        s = {n: sem(n) for n in names}
        main_loaded = sem("main_loaded")

        with nc.Block() as block:
            @block.sync
            def _(sp):
                loads = ((consts[:], table),
                         (Wo[:], woT.rearrange("(c p) n -> p c n", p=P)),
                         (mix[:, 0:1], mu_r), (mix[:, 1:2], mu_k))
                for dst, src in loads:
                    sp.dma_start(dst, src).then_inc(main_loaded, 16)
                sp.wait_ge(main_loaded, 16 * len(loads))

            @block.vector
            def _(dve):
                dve.memset(ones[:], 1.0)
                dve.memset(eps[:], EPS)
                dve.memset(V[:, :, :, DH:DH + 1], 1.0)
                dve.wait_ge(main_loaded, 64)
                dve.tensor_copy(ident16[:], ident)
                dve.tensor_copy(mask16[:], consts[:, C_MASK:C_MASK + P])
                dve.tensor_scalar(mix[:, 2:4], mix[:, 0:2], -1.0, 1.0, ALU.mult, ALU.add)

        x_rows = x.rearrange("b (t p) c -> b p t c", p=P)
        out_rows = out.rearrange("b (t p) c -> b p t c", p=P)

        with nc.Fori(0, B) as b:
            with nc.Block() as block:
                @block.sync
                def _(sp):
                    sp.dma_start(xin, x_rows[b]).then_inc(s["x_loaded"], 16)
                    for dst, src in ((Wq, wqT), (Wk, wkT), (Wv, wvT), (Wr, wrT), (Wkf, wkfT), (Wvf, wvfT)):
                        sp.dma_start(dst, src).then_inc(s["tables_loaded"], 16)
                    for i in range(4):
                        sp.dma_start(rot[i], rotary[:, i * 512:(i + 1) * 512]).then_inc(s["tables_loaded"], 16)
                    sp.wait_ge(s["tables_loaded"], 160)

                @block.gpsimd
                def _(pool):
                    pool.memset(krow, 0.0).then_inc(s["p_pad"], 1)
                    pool.memset(gram, 0.0).then_inc(s["p_pad"], 1)
                    for t in range(TILES):
                        pool.wait_ge(s["p_rope"], t + 1)
                        if t:
                            pool.wait_ge(s["p_stats_read"], 4 * t)
                            pool.wait_ge(s["p_qT"], 8 * t)
                        pool.tensor_tensor(qrow[:, 0, :], qcos[:, 0, :], qsin[:, 0, :], ALU.add).then_inc(s["p_kvcopied"], 1)

                @block.vector
                def _(dve):
                    n = [0]

                    def link(ins):
                        n[0] += 1
                        ins.then_inc(s["dve_step"], 1)
                        dve.wait_ge(s["dve_step"], n[0])
                    dve.wait_ge(s["x_loaded"], 16)
                    for t in range(TILES):
                        link(dve.bn_stats(bn[:, t, :], xin[:, t, :]))
                        link(dve.bn_aggr(mv[:, t, :], bn[:, t, :]))
                    dve.tensor_copy(rstd, mv[:, :, 1]).then_inc(s["p_stat"], 1)
                    dve.wait_ge(s["p_std"], 1)
                    link(dve.reciprocal(rstd, std))
                    for t in range(TILES):
                        dve.tensor_scalar(xn[:, t, :], xin[:, t, :], mv[:, t, 0:1], rstd[:, t:t + 1],
                                          ALU.subtract, ALU.mult).then_inc(s["p_xn"], 1)
                    dve.wait_ge(s["p_xnT"], TILES)
                    dve.tensor_copy(xnT[:, 0:BANK], psum[:, 0, :]).then_inc(s["p_xnT_read"], 1)
                    dve.tensor_copy(xnT[:, BANK:S], psum[:, 1, :]).then_inc(s["p_xnT_read"], 1)
                    dve.wait_ge(s["p_pad"], 2)
                    dve.wait_ge(s["tables_loaded"], 160)
                    for t in range(TILES):
                        cos = [r[:, t * DH:(t + 1) * DH] for r in rot]
                        dve.wait_ge(s["p_proj"], t + 1)
                        if t:
                            dve.wait_ge(s["p_kvcopied"], t)
                            dve.wait_ge(s["p_gram"], t)
                            dve.wait_ge(s["p_kT"], 2 * t)
                        for half in range(2):
                            q = psum[:, half, :].rearrange("p (h d) -> p h d", d=DH)
                            oc = qcos[:, 0, half * BANK:(half + 1) * BANK].rearrange("p (h d) -> p h d", d=DH)
                            os = qsin[:, 0, half * BANK:(half + 1) * BANK].rearrange("p (h d) -> p h d", d=DH)
                            dve.tensor_tensor(oc, q, cos[0].unsqueeze(1).to_broadcast([P, 8, DH]), ALU.mult)
                            dve.tensor_tensor(os[:, :, 0:32], q[:, :, 32:64],
                                              cos[1][:, 0:32].unsqueeze(1).to_broadcast([P, 8, 32]), ALU.mult)
                            last = dve.tensor_tensor(os[:, :, 32:64], q[:, :, 0:32],
                                                     cos[1][:, 32:64].unsqueeze(1).to_broadcast([P, 8, 32]), ALU.mult)
                        last.then_inc(s["p_rope"], 1)
                        k = psum[:, 2, 0:256].rearrange("p (h d) -> p h d", d=DH)
                        kc = kcos.rearrange("p (h d) -> p h d", d=DH)
                        ks = ksin.rearrange("p (h d) -> p h d", d=DH)
                        dve.tensor_tensor(kc, k, cos[2].unsqueeze(1).to_broadcast([P, KV, DH]), ALU.mult)
                        dve.tensor_tensor(ks[:, :, 0:32], k[:, :, 32:64],
                                          cos[3][:, 0:32].unsqueeze(1).to_broadcast([P, KV, 32]), ALU.mult)
                        dve.tensor_tensor(ks[:, :, 32:64], k[:, :, 0:32],
                                          cos[3][:, 32:64].unsqueeze(1).to_broadcast([P, KV, 32]), ALU.mult)
                        link(dve.tensor_copy(V[:, t, :, 0:DH], psum[:, 2, 256:512].rearrange("p (h d) -> p h d", d=DH)))
                        dve.tensor_tensor(krow[:, :, 64:128], kc, ks, ALU.add).then_inc(s["p_proj_read"], 1)
                        dve.wait_ge(s["p_gram"], t + 1)
                        for half in range(2):
                            link(dve.tensor_tensor(gram[:, 2 * half:2 * half + 2, :], gram[:, 2 * half:2 * half + 2, :],
                                                   psum[:, 4 + half, 0:260].rearrange("p (k c) -> p k c", k=2), ALU.add))
                        dve.memset(rden[:, 0:1], 1.0).then_inc(s["p_gram_read"], 1)
                        for quad in range(4):
                            dve.wait_ge(s["p_stats"], 4 * t + quad + 1)
                            st = psum[:, 6 + quad % 2, 0:260].rearrange("p (h c) -> p h c", h=4)
                            link(dve.tensor_tensor(prod[:, 0:256].rearrange("p (h d) -> p h d", h=4), st[:, :, 0:64],
                                                   qrow[:, 0, quad * 256:(quad + 1) * 256].rearrange("p (h d) -> p h d", h=4),
                                                   ALU.mult))
                            dve.tensor_reduce(ssq[:, t, 4 * quad:4 * quad + 4],
                                              prod[:, 0:256].rearrange("p (h d) -> p h d", h=4), AXIS.X, ALU.add)
                            link(dve.tensor_copy(ssum[:, t, 4 * quad:4 * quad + 4], st[:, :, 64]))
                            dve.memset(rden[:, 1:2], 1.0).then_inc(s["p_stats_read"], 1)
                    for t in range(TILES):
                        link(dve.tensor_scalar(mean[:, t, :], ssum[:, t, :], 1.0 / ((t + 1) * P), None, ALU.mult))
                        link(dve.tensor_scalar(ssq[:, t, :], ssq[:, t, :], 1.0 / ((t + 1) * P), None, ALU.mult))
                    link(dve.tensor_tensor(var, mean, mean, ALU.mult))
                    link(dve.tensor_tensor(var, ssq, var, ALU.subtract))
                    dve.tensor_scalar(var, var, 0.0, None, ALU.max).then_inc(s["p_var"], 1)
                    dve.wait_ge(s["p_kvcopied"], TILES)
                    link(dve.memset(prevT[:, 0:1], 0.0))
                    link(dve.tensor_copy(prevT[:, 1:S], xnT[:, 0:S - 1]))
                    link(dve.tensor_scalar(xrT, xnT, mix[:, 0:1], None, ALU.mult))
                    link(dve.tensor_scalar(xkT, xnT, mix[:, 1:2], None, ALU.mult))
                    dve.scalar_tensor_tensor(xrT, prevT, mix[:, 2:3], xrT, ALU.mult, ALU.add).then_inc(s["p_mixed"], 1)
                    dve.scalar_tensor_tensor(xkT, prevT, mix[:, 3:4], xkT, ALU.mult, ALU.add).then_inc(s["p_mixed"], 1)
                    dve.wait_ge(s["p_dev"], 1)
                    for t in range(TILES):
                        link(dve.scalar_tensor_tensor(base[:, t, :], dev[:, t, :], consts[:, C_Z + t:C_Z + t + 1],
                                                      mean[:, t, :], ALU.mult, ALU.add))
                        link(dve.tensor_scalar(slope[:, t, :], dev[:, t, :], consts[:, C_STEP + t:C_STEP + t + 1],
                                               None, ALU.mult))
                    dve.wait_ge(s["p_relu"], 2)
                    dve.tensor_tensor(kact, relu, relu, ALU.mult).then_inc(s["p_kact"], 1)
                    dve.wait_ge(s["p_exp"], 2)
                    link(dve.tensor_scalar(gden, gate, 1.0, None, ALU.add))
                    link(dve.reciprocal(gate, gden))
                    dve.wait_ge(s["p_v"], 1)
                    for half in range(2):
                        sl = slice(half * BANK, (half + 1) * BANK)
                        link(dve.tensor_tensor(gden[:, sl], gate[:, sl], psum[:, 4 + half, :], ALU.mult))
                    link(dve.tensor_tensor(resid[:].rearrange("p t c -> p (t c)"), gden,
                                           xin.rearrange("p t c -> p (t c)"), ALU.add))

                @block.scalar
                def _(act):
                    act.wait_ge(s["p_stat"], 1)
                    act.activation(std, rstd, ACT.Sqrt, bias=eps[:, 0:1]).then_inc(s["p_std"], 1)
                    for t in range(TILES):
                        for half in range(2):
                            act.wait_ge(s["p_qT"], 8 * t + 4 * half + 4)
                            act.activation(QT[:, 4 * half:4 * half + 4, t * P:(t + 1) * P],
                                           psum[:, 3, :].rearrange("p (a c) -> p a c", a=4), ACT.Copy)\
                               .then_inc(s["p_qT_read"], 1)
                        for half in range(2):
                            act.wait_ge(s["p_kT"], 2 * t + half + 1)
                            act.activation(KT[:, 2 * half:2 * half + 2, :, t * P:(t + 1) * P],
                                           psum[:, 3, :].rearrange("p (a v c) -> p a v c", a=2, v=2), ACT.Copy)\
                               .then_inc(s["p_kT_read"], 1)
                    act.wait_ge(s["p_var"], 1)
                    act.activation(dev, var, ACT.Sqrt).then_inc(s["p_dev"], 1)
                    act.wait_ge(s["p_ffn"], 1)
                    for half in range(2):
                        act.activation(relu[:, half * BANK:(half + 1) * BANK], psum[:, half, :], ACT.Relu)\
                           .then_inc(s["p_relu"], 1)
                    act.wait_ge(s["p_ffn"], 2)
                    for half in range(2):
                        act.activation(gate[:, half * BANK:(half + 1) * BANK], psum[:, 2 + half, :], ACT.Exp, scale=-1.0)\
                           .then_inc(s["p_exp"], 1)

                @block.tensor
                def _(pe):
                    for t in range(TILES):
                        pe.wait_ge(s["p_xn"], t + 1)
                        pe.transpose(psum[:, t // 4, (t % 4) * P:(t % 4 + 1) * P], xn[:, t, :], ident)\
                          .then_inc(s["p_xnT"], 1)
                    pe.wait_ge(s["p_xnT_read"], 2)
                    pe.wait_ge(s["tables_loaded"], 160)
                    for t in range(TILES):
                        if t:
                            pe.wait_ge(s["p_proj_read"], t)
                        xt = xnT[:, t * P:(t + 1) * P]
                        pe.matmul(psum[:, 0, :], xt, Wq[:, 0:BANK], start=True, stop=True)
                        pe.matmul(psum[:, 1, :], xt, Wq[:, BANK:2 * BANK], start=True, stop=True)
                        pe.matmul(psum[:, 2, 0:256], xt, Wk, start=True, stop=True)
                        pe.matmul(psum[:, 2, 256:512], xt, Wv, start=True, stop=True).then_inc(s["p_proj"], 1)
                        pe.wait_ge(s["p_proj_read"], t + 1)
                        pe.wait_ge(s["p_kvcopied"], t + 1)
                        for half in range(2):
                            if t and half == 0:
                                pe.wait_ge(s["p_kT_read"], 2 * t)
                            if t or half:
                                pe.wait_ge(s["p_qT_read"], 2 * t + half)
                            for a in range(4):
                                pair = 4 * half + a
                                pe.transpose(psum[:, 3, a * P:(a + 1) * P], qrow[:, 0, pair * P:(pair + 1) * P], ident)\
                                  .then_inc(s["p_qT"], 1)
                        for half in range(2):
                            if half == 0:
                                pe.wait_ge(s["p_qT_read"], 2 * t + 2)
                            else:
                                pe.wait_ge(s["p_kT_read"], 2 * t + 1)
                            for a in range(2):
                                kv = 2 * half + a
                                pe.transpose(psum[:, 3, (2 * a) * P:(2 * a + 1) * P], krow[:, kv, 64:192], ident)
                                last = pe.transpose(psum[:, 3, (2 * a + 1) * P:(2 * a + 2) * P], krow[:, kv, 0:128], ident)
                            last.then_inc(s["p_kT"], 1)
                        if t:
                            pe.wait_ge(s["p_gram_read"], t)
                        for kv in range(KV):
                            g = psum[:, 4 + kv // 2, (kv % 2) * 130:(kv % 2) * 130 + 130]
                            for v in range(2):
                                lhs = krow[:, kv, 64:192] if v == 0 else krow[:, kv, 0:128]
                                pe.matmul(g[:, 65 * v:65 * v + 64], lhs, krow[:, kv, 64:128], start=True, stop=True)
                                last = pe.matmul(g[:, 65 * v + 64:65 * v + 65], lhs, ones[:], start=True, stop=True)
                        last.then_inc(s["p_gram"], 1)
                        pe.wait_ge(s["p_gram_read"], t + 1)
                        for quad in range(4):
                            i = 4 * t + quad
                            if i >= 2:
                                pe.wait_ge(s["p_stats_read"], i - 1)
                            for a in range(2):
                                pair = 2 * quad + a
                                last = pe.matmul(psum[:, 6 + quad % 2, 130 * a:130 * a + 130],
                                                 QT[:, pair, t * P:(t + 1) * P], gram[:, quad, :], start=True, stop=True)
                            last.then_inc(s["p_stats"], 1)
                    pe.wait_ge(s["p_mixed"], 2)
                    pe.wait_ge(s["p_kT_read"], 2 * TILES)
                    for half in range(2):
                        last = pe.matmul(psum[:, half, :], Wkf, xkT[:, half * BANK:(half + 1) * BANK], start=True, stop=True)
                    last.then_inc(s["p_ffn"], 1)
                    for t in range(TILES):
                        last = pe.matmul(psum[:, 2 + t // 4, (t % 4) * P:(t % 4 + 1) * P], xrT[:, t * P:(t + 1) * P], Wr,
                                         start=True, stop=True)
                    last.then_inc(s["p_ffn"], 1)
                    pe.wait_ge(s["p_kact"], 1)
                    for t in range(TILES):
                        last = pe.matmul(psum[:, 4 + t // 4, (t % 4) * P:(t % 4 + 1) * P], kact[:, t * P:(t + 1) * P], Wvf,
                                         start=True, stop=True)
                    last.then_inc(s["p_v"], 1)

            def key_tiles(k):
                return GROUPS[k][0] + 1

            def live(k):
                return 0 <= k < NG

            def ends_tile(k):
                return live(k) and GROUPS[k][1] == KV - 1

            bank, room, uses, banks, rooms = {}, {}, [], 0, 0
            for rnd in range(NG + 5):
                if live(rnd - 2):
                    bank["weights", rnd - 2], room["weights", rnd - 2] = banks, rooms
                    banks, rooms = banks + key_tiles(rnd - 2), rooms + key_tiles(rnd - 2)
                    uses += [(uses[-1] if uses else 0) + 1 + i for i in range(key_tiles(rnd - 2))]
                if ends_tile(rnd - 4):
                    bank["heads", rnd - 4], room["heads", rnd - 4] = banks, rooms
                    banks, rooms = banks + 3, rooms + 2
                    uses += [(uses[-1] if uses else 0) + 1] * 2

            with nc.Block() as block:
                @block.tensor
                def _(pe):
                    def scores(k, j):
                        t, kv = GROUPS[k]
                        u, h, L = GROUP * k + j, GROUP * kv + j, (t + 1) * P
                        if u >= 2:
                            pe.wait_ge(s["scores_read"], u - 1)
                        for c in range(0, L, BANK):
                            w = min(BANK, L - c)
                            bank = psum[:, 2 * (u % 2) + c // BANK, :]
                            diagonal = c + w == L
                            pe.matmul(bank[:, 0:w], QT[:, h // 2, t * P:(t + 1) * P], KT[:, kv, h % 2, c:c + w],
                                      start=True, stop=not diagonal)
                            if diagonal:
                                pe.matmul(bank[:, w - P:w], ident16[:], mask16[:], start=False, stop=True)\
                                  .then_inc(s["scores_done"], 1)

                    def transposes(k, i):
                        q = bank["weights", k] + i
                        if q >= 2:
                            pe.wait_ge(s["chunk_read"], q - 1)
                        for j in range(GROUP):
                            if i == 0:
                                pe.wait_ge(s["weight_ready"], GROUP * k + j + 1)
                            last = pe.transpose(psum[:, 4 + q % 2, j * P:(j + 1) * P],
                                                weight[:, k % RING, j, i * P:(i + 1) * P], ident)
                        last.then_inc(s["chunk_done"], 1)

                    def products(k, i):
                        t, kv = GROUPS[k]
                        pe.wait_ge(s["chunk_read"], bank["weights", k] + i + 1)
                        if i == 0 and k:
                            pe.wait_ge(s["sums_read"], k)
                        pe.matmul(psum[0:DH + 1, 6, :], V[:, i, kv, :], PT[:, (room["weights", k] + i) % PTS, :],
                                  start=(i == 0), stop=(i == t)).then_inc(s["chunk_used"], 1)

                    def back(k):
                        pe.wait_ge(s["sums_read"], k + 1)
                        pe.wait_ge(s["out_read"], k)
                        pe.wait_ge(s["fail_read"], min(k + 2, NG))
                        for j in range(GROUP):
                            last = pe.transpose(psum[:, 7, j * (DH + 1):(j + 1) * (DH + 1)], outT[:, j * P:(j + 1) * P],
                                                ident[0:DH + 1, 0:DH + 1])
                        last.then_inc(s["back_done"], 1)

                    def sum_fails(k):
                        pe.wait_ge(s["fail_ready"], k + 1)
                        if k >= 3:
                            pe.wait_ge(s["out_read"], k - 2)
                        if k:
                            pe.wait_ge(s["fail_read"], k)
                        pe.matmul(psum[0:1, 7, 320:320 + GROUP + 1], ones[:], fail[:], start=True, stop=True)\
                          .then_inc(s["fail_summed"], 1)

                    def project(k):
                        q = bank["heads", k]
                        pe.wait_ge(s["out_read"], k + 1)
                        for i in range(2):
                            pe.wait_ge(s["chunk_read"], q + i - 1)
                            for a in range(4):
                                last = pe.transpose(psum[:, 4 + (q + i) % 2, a * P:(a + 1) * P],
                                                    heads_out[:, (4 * i + a) * P:(4 * i + a + 1) * P], ident)
                            last.then_inc(s["chunk_done"], 1)
                        for i in range(2):
                            pe.wait_ge(s["chunk_read"], q + i + 1)
                            for a in range(4):
                                last = pe.matmul(psum[:, 4 + q % 2, 0:D], PT[:, (room["heads", k] + i) % PTS, a * P:(a + 1) * P],
                                                 Wo[:, 4 * i + a, :], start=(i + a == 0), stop=(i + a == 4))
                            last.then_inc(s["chunk_used"] if i == 0 else s["chunk_done"], 1)

                    for j in range(GROUP):
                        scores(0, j)
                    for j in range(2):
                        scores(1, j)
                    for rnd in range(NG + 5):
                        k = rnd - 2
                        if live(k):
                            transposes(k, 0)
                            for i in range(key_tiles(k)):
                                if i + 1 < key_tiles(k):
                                    transposes(k, i + 1)
                                products(k, i)
                        if live(rnd - 3):
                            back(rnd - 3)
                        if live(rnd - 1):
                            sum_fails(rnd - 1)
                        for k, j in ((rnd + 1, 2), (rnd + 1, 3), (rnd + 2, 0), (rnd + 2, 1)):
                            if live(k):
                                scores(k, j)
                        if ends_tile(rnd - 4):
                            project(rnd - 4)

                @block.scalar
                def _(act):
                    n = [0]

                    def signs(k, tau, acc, counted, between):
                        L = key_tiles(k) * P
                        for j in range(GROUP):
                            if n[0] >= 2:
                                act.wait_ge(s["act_step"], n[0] - 1)
                            act.activation(junk[:, n[0] % 2, 0:L], depth[:, k % DRING, j, 0:L], ACT.Sign,
                                           bias=tau[:, k % SR, j:j + 1], scale=-1.0, accum_out=acc[:, k % SR, j:j + 1])\
                               .then_inc(s["act_step"], 1)
                            n[0] += 1
                            between(j)
                        act.wait_ge(s["act_step"], n[0])
                        act.activation(acc[:, k % SR, :], acc[:, k % SR, :], ACT.Copy).then_inc(counted, 1)

                    def keep(q, m):
                        act.wait_ge(s["chunk_done"], q + 1)
                        if m >= PTS:
                            act.wait_ge(s["chunk_used"], uses[m - PTS])
                        act.activation(PT[:, m % PTS, :], psum[:, 4 + q % 2, :], ACT.Copy).then_inc(s["chunk_read"], 1)

                    for rnd in range(NG + 6):
                        k = rnd - 5
                        if ends_tile(k):
                            act.wait_ge(s["chunk_done"], bank["heads", k] + 3)
                            if k >= KV:
                                act.wait_ge(s["y_read"], k // KV)
                            act.activation(attn_out[:], psum[:, 4 + bank["heads", k] % 2, 0:D], ACT.Copy)\
                               .then_inc(s["chunk_read"], 1)
                        k = rnd - 3
                        if live(k):
                            act.wait_ge(s["chunk_used"], uses[room["weights", k] + key_tiles(k) - 1])
                            if k:
                                act.wait_ge(s["back_done"], k)
                            act.activation(outT[:], psum[0:DH + 1, 6, :], ACT.Copy).then_inc(s["sums_read"], 1)
                        k = rnd - 2
                        todo = [(bank["weights", k] + i, room["weights", k] + i) for i in range(key_tiles(k))] if live(k) else []

                        def chunks_left(left):
                            while len(todo) > max(left, 0):
                                keep(*todo.pop(0))
                        k = rnd
                        if live(k):
                            L = key_tiles(k) * P
                            act.wait_ge(s["tau1_ready"], k + 1)
                            signs(k, tau1, sign1, s["count1"], lambda j: chunks_left(7 - j // 2))
                            if k >= RING:
                                act.wait_ge(s["chunk_done"], bank["weights", k - RING] + key_tiles(k - RING))
                            for j in range(GROUP):
                                act.activation(weight[:, k % RING, j, 0:L], depth[:, k % DRING, j, 0:L], ACT.Exp, scale=-1.0)\
                                   .then_inc(s["exp_ready"], 1)
                                chunks_left(5 - j)
                            act.wait_ge(s["tau2_ready"], k + 1)
                            signs(k, tau2, sign2, s["count2"], lambda j: chunks_left(1 - j))
                            act.wait_ge(s["tau3_ready"], k + 1)
                            signs(k, tau3, sign3, s["count3"], lambda j: None)
                        chunks_left(0)
                        k = rnd - 4
                        if ends_tile(k):
                            for i in range(2):
                                keep(bank["heads", k] + i, room["heads", k] + i)

                @block.gpsimd
                def _(pool):
                    n = [0]

                    def link(ins):
                        n[0] += 1
                        ins.then_inc(s["pool_step"], 1)
                        pool.wait_ge(s["pool_step"], n[0])

                    def missing(k, acc):
                        t, kv = GROUPS[k]
                        link(pool.tensor_scalar(step_a[:], acc[:, k % SR, :], -0.5, consts[:, C_AIM + t:C_AIM + t + 1],
                                                ALU.mult, ALU.add))
                        link(pool.tensor_tensor(step_b[:], step_a[:], slope[:, t, GROUP * kv:GROUP * (kv + 1)], ALU.mult))

                    def second(k):
                        pool.wait_ge(s["count1"], k + 1)
                        missing(k, sign1)
                        pool.tensor_tensor(tau2[:, k % SR, :], tau1[:, k % SR, :], step_b[:], ALU.add)\
                            .then_inc(s["tau2_ready"], 1)

                    def third(k):
                        t, kv = GROUPS[k]
                        L = (t + 1) * P
                        pool.wait_ge(s["count2"], k + 1)
                        pool.wait_ge(s["tau2_ready"], k + 1)
                        missing(k, sign2)
                        link(pool.tensor_scalar(step_c[:], sign2[:, k % SR, :], float(2 * TOPK - L), None, ALU.is_lt))
                        link(pool.tensor_scalar(step_d[:], sign2[:, k % SR, :], float(2 * (TOPK + WINDOW) - L), None, ALU.is_ge))
                        link(pool.tensor_tensor(step_c[:], step_c[:], step_d[:], ALU.add))
                        link(pool.tensor_tensor(step_b[:], step_b[:], step_c[:], ALU.mult))
                        pool.tensor_tensor(tau3[:, k % SR, :], tau2[:, k % SR, :], step_b[:], ALU.add)\
                            .then_inc(s["tau3_ready"], 1)

                    def ranks(k):
                        L = (GROUPS[k][0] + 1) * P
                        pool.wait_ge(s["count3"], k + 1)
                        pool.wait_ge(s["tau3_ready"], k + 1)
                        link(pool.tensor_scalar(rank[:, k % SR, :], sign3[:, k % SR, :], 0.5, float(L / 2 - TOPK),
                                                ALU.mult, ALU.add))
                        link(pool.tensor_scalar(step_c[:], rank[:, k % SR, :], 0.0, None, ALU.is_lt))
                        link(pool.tensor_scalar(step_d[:], rank[:, k % SR, :], float(WINDOW - 1), None, ALU.is_gt))
                        pool.tensor_tensor(outside[:, k % SR, :], step_c[:], step_d[:], ALU.add).then_inc(s["rank_ready"], 1)

                    def depths(k):
                        t, kv = GROUPS[k]
                        L = (t + 1) * P
                        for j in range(GROUP):
                            pool.wait_ge(s["scores_read"], GROUP * k + j + 1)
                            d = depth[:, k % DRING, j, 0:L]
                            pool.tensor_scalar(d, d, -1.0, rowmax[:, k % SR, j:j + 1], ALU.mult, ALU.add)\
                                .then_inc(s["depth_ready"], 1)
                        pool.tensor_tensor(tau1[:, k % SR, :], rowmax[:, k % SR, :], base[:, t, GROUP * kv:GROUP * (kv + 1)],
                                           ALU.subtract).then_inc(s["tau1_ready"], 1)

                    def finish(k):
                        pool.wait_ge(s["chunk_read"], bank["heads", k] + 3)
                        if k >= KV:
                            pool.wait_ge(s["stored"], 16 * (k // KV))
                        pool.tensor_tensor(yout[:], attn_out[:], resid[:, GROUPS[k][0], :], ALU.add).then_inc(s["y_read"], 1)

                    for rnd in range(NG + 6):
                        if ends_tile(rnd - 5):
                            finish(rnd - 5)
                        if live(rnd):
                            depths(rnd)
                            second(rnd)
                            third(rnd)
                            ranks(rnd)

                @block.vector
                def _(dve):
                    n = [0]

                    def link(ins):
                        n[0] += 1
                        ins.then_inc(s["thr_step"], 1)
                        dve.wait_ge(s["thr_step"], n[0])

                    def mark(ins):
                        n[0] += 1
                        ins.then_inc(s["thr_step"], 1)
                        return n[0]

                    def take_scores(k, heads):
                        L = key_tiles(k) * P
                        for j in heads:
                            u = GROUP * k + j
                            dve.wait_ge(s["scores_done"], u + 1)
                            if k >= DRING:
                                dve.wait_ge(s["weight_ready"], GROUP * (k - DRING) + j + 1)
                            dve.tensor_scalar(depth[:, k % DRING, j, 0:L],
                                              psum[:, 2 * (u % 2):2 * (u % 2) + 2, :].rearrange("p a c -> p (a c)")[:, 0:L],
                                              1.0, None, ALU.mult, ALU.max, accum_out=rowmax[:, k % SR, j:j + 1])\
                               .then_inc(s["scores_read"], 1)

                    def thresholds(k):
                        t, kv = GROUPS[k]
                        L = (t + 1) * P
                        w = L // SEGMENTS
                        heads = range(GROUP)
                        dve.wait_ge(s["rank_ready"], k + 1)

                        def select(j):
                            d = depth[:, k % DRING, j, 0:L]
                            return mark(dve.scalar_tensor_tensor(zbuf[:, j % 2, 0:L], d, tau3[:, k % SR, j:j + 1], d,
                                                                 ALU.is_le, ALU.mult))
                        selected, found = {0: select(0), 1: select(1)}, {}
                        for j in heads:
                            dve.wait_ge(s["thr_step"], selected[j])
                            for g in range(SEGMENTS):
                                last = dve.max(cand[:, j, g, :], zbuf[:, j % 2, g * w:(g + 1) * w])
                            found[j] = mark(last)
                            if 1 <= j < 3:
                                dve.wait_ge(s["thr_step"], found[j - 1])
                                selected[j + 1] = select(j + 1)
                        flat = [cand[:, j, :, :].rearrange("p a c -> p (a c)") for j in heads]
                        source, done = flat, [found[j] for j in heads]
                        for lot in range(WINDOW // 8):
                            for j in heads:
                                dve.wait_ge(s["thr_step"], done[j])
                                done[j] = mark(dve.max(sorted24[:, j, 8 * lot:8 * lot + 8], source[j]))
                            if lot + 1 < WINDOW // 8:
                                for j in heads:
                                    dve.wait_ge(s["thr_step"], done[j])
                                    done[j] = mark(dve.match_replace(rest[:, j, :], sorted24[:, j, 8 * lot:8 * lot + 8],
                                                                     source[j], -1.0))
                                source = [rest[:, j, :] for j in heads]
                        for j in heads:
                            dve.wait_ge(s["thr_step"], done[j])
                            done[j] = mark(dve.scalar_tensor_tensor(pick[:, j, :], consts[:, C_RANK:C_RANK + WINDOW],
                                                                    rank[:, k % SR, j:j + 1], sorted24[:, j, :],
                                                                    ALU.is_equal, ALU.mult, accum_out=thr[:, k % 2, j:j + 1]))
                        if k:
                            dve.wait_ge(s["fail_summed"], k)
                        link(dve.tensor_reduce(segmin[:], cand[:, :, :, 7], AXIS.X, ALU.max))
                        mark(dve.tensor_tensor(fail_c[:], sorted24[:, :, 0], tau3[:, k % SR, :], ALU.is_equal))
                        link(dve.tensor_tensor(fail_b[:], segmin[:], thr[:, k % 2, :], ALU.is_gt))
                        link(dve.tensor_tensor(fail_b[:], fail_b[:], outside[:, k % SR, :], ALU.add))
                        link(dve.tensor_tensor(fail[:, 0:GROUP], fail_c[:], fail_b[:], ALU.add))
                        if t == 0:
                            link(dve.tensor_scalar(fail[:, 0:GROUP], fail[:, 0:GROUP], consts[:, C_SEARCHED:C_SEARCHED + 1],
                                                   None, ALU.mult))
                            link(dve.tensor_scalar(thr[:, k % 2, :], thr[:, k % 2, :], consts[:, C_OPEN:C_OPEN + 1],
                                                   None, ALU.max))
                        dve.tensor_reduce(fail[:, GROUP:GROUP + 1], fail[:, 0:GROUP], AXIS.X, ALU.add)\
                           .then_inc(s["fail_ready"], 1)

                    def exact_head(k, j):
                        t, kv = GROUPS[k]
                        L = (t + 1) * P
                        m = [0]
                        dve.sem_clear(s["slow_step"])

                        def then(ins):
                            m[0] += 1
                            ins.then_inc(s["slow_step"], 1)
                            dve.wait_ge(s["slow_step"], m[0])
                        then(dve.tensor_scalar(slow[:, 0:L], depth[:, k % DRING, j, 0:L], -1.0, None, ALU.mult))
                        for i in range(TOPK // 8):
                            then(dve.max(best8[:], slow[:, 0:L]))
                            if i + 1 < TOPK // 8:
                                then(dve.match_replace(slow[:, 0:L], best8[:], slow[:, 0:L], -BIG))
                        found = thr[:, k % 2, j:j + 1]
                        then(dve.tensor_scalar(found, best8[:, 7:8], -1.0, None, ALU.mult))
                        if t == 0:
                            then(dve.tensor_scalar(found, found, consts[:, C_OPEN:C_OPEN + 1], None, ALU.max))

                    def take_failures(k):
                        dve.wait_ge(s["fail_summed"], k + 1)
                        dve.tensor_copy(failed[:], psum[0:1, 7, 320:320 + GROUP + 1]).then_inc(s["fail_read"], 1)

                    def failures(column):
                        return dve.value_load(failed[0:1, column:column + 1], min_val=0, max_val=GROUP * P * GROUP)

                    def exact(k):
                        dve.wait_ge(s["fail_read"], k + 1)
                        with dve.If(failures(GROUP) > 0):
                            for j in range(GROUP):
                                with dve.If(failures(j) > 0):
                                    exact_head(k, j)

                    def weights(k):
                        L = key_tiles(k) * P
                        dve.wait_ge(s["exp_ready"], GROUP * (k + 1))
                        for j in range(GROUP):
                            e = weight[:, k % RING, j, 0:L]
                            dve.scalar_tensor_tensor(e, depth[:, k % DRING, j, 0:L], thr[:, k % 2, j:j + 1], e,
                                                     ALU.is_le, ALU.mult).then_inc(s["weight_ready"], 1)

                    def normalise(k):
                        t, kv = GROUPS[k]
                        dve.wait_ge(s["back_done"], k + 1)
                        sums = psum[:, 7, 0:GROUP * (DH + 1)].rearrange("p (h d) -> p h d", d=DH + 1)
                        link(dve.reciprocal(rden[:], sums[:, :, DH]))
                        if kv == 0 and k:
                            dve.wait_ge(s["chunk_done"], bank["heads", k - 1] + 2)
                        dve.tensor_tensor(heads_out[:, kv * 256:(kv + 1) * 256].rearrange("p (h d) -> p h d", d=DH),
                                          sums[:, :, 0:DH], rden[:].unsqueeze(2).to_broadcast([P, GROUP, DH]), ALU.mult)\
                           .then_inc(s["out_read"], 1)

                    take_scores(0, range(GROUP))
                    for rnd in range(NG + 5):
                        if live(rnd - 4):
                            normalise(rnd - 4)
                        if live(rnd - 1):
                            thresholds(rnd - 1)
                        if live(rnd + 1):
                            take_scores(rnd + 1, (0,))
                        if live(rnd - 1):
                            take_failures(rnd - 1)
                        if live(rnd + 1):
                            take_scores(rnd + 1, (1,))
                        if live(rnd - 1):
                            exact(rnd - 1)
                            weights(rnd - 1)
                        if live(rnd + 1):
                            take_scores(rnd + 1, (2, 3))

                @block.sync
                def _(sp):
                    for i, t in enumerate(ORDER):
                        sp.wait_ge(s["y_read"], i + 1)
                        sp.dma_start(out_rows[b, :, t, :], yout[:]).then_inc(s["stored"], 16)
                    sp.wait_ge(s["stored"], 16 * TILES)

            with nc.Block() as block:
                @block.sync
                def _(sp):
                    for one in s.values():
                        sp.sem_clear(one)


def kernel(**inputs):
    import concourse.bacc as bacc
    from concourse.bass_utils import run_bass_kernel_spmd
    a = {n.split("L0_")[1]: np.asarray(v) for n, v in inputs.items()}
    arrays = {
        "x": a["attn_x"], "wqT": a["attn_Wq"].T, "wkT": a["attn_Wk"].T, "wvT": a["attn_Wv"].T, "woT": a["attn_Wo"].T,
        "wrT": a["ffn_W_r"].T, "wkfT": a["ffn_W_k"].T, "wvfT": a["ffn_W_v"].T,
        "mu_r": a["ffn_mu_r"].reshape(P, 1), "mu_k": a["ffn_mu_k"].reshape(P, 1), 
    }
    arrays["table"], arrays["rotary"] = constant_tables()
    arrays = {n: np.ascontiguousarray(v) for n, v in arrays.items()}
    nc = bacc.Bacc("TRN2", target_bir_lowering=False, num_devices=1)
    args = {n: nc.dram_tensor(n, v.shape, F32, kind="ExternalInput").ap() for n, v in arrays.items()}
    out = nc.dram_tensor("out", (B, S, D), F32, kind="ExternalOutput").ap()
    build(nc, out=out, **args)
    return run_bass_kernel_spmd(nc, [arrays], core_ids=[0]).results[0]["out"]
```

```python
import math
from contextlib import ExitStack

import numpy as np
import concourse.bass as bass
from concourse import mybir

F32 = mybir.dt.float32
BF16 = mybir.dt.bfloat16
I32 = mybir.dt.int32
ALU = mybir.AluOpType
ACT = mybir.ActivationFunctionType
AXIS = mybir.AxisListType

B, S, D = 2, 1024, 128
HEADS, KV, DH = 16, 4, 64
GROUP = HEADS // KV
PAIRS = HEADS // 2
P = 128
TILES = S // P
TOPK = 64
NEG = -1e30
EPS = 1e-5
BANK = 512

AIM_FIRST, AIM = 69.0, 72.0
WINDOW = 24
SEGMENTS = 8
BIG = 3e38

C_IDENT, C_MASK, C_RANK = 0, 128, 256
C_Z, C_STEP, C_AIM = 288, 296, 304
C_OPEN, C_SEARCHED, C_INV = 312, 313, 314
C_WIDTH = C_INV + TILES
R_COSQ, R_SINQ, R_COSK, R_SINK = 0, 512, 1024, 1536

ORDER = list(range(TILES - 1, -1, -1))
GROUPS = [(t, kv) for t in ORDER for kv in range(KV)]
NG = len(GROUPS)
RING = 3
PTS = 3
DRING = 3


def density(z):
    return math.exp(-z * z / 2) / math.sqrt(2 * math.pi)


def deviate(share):
    low, high = -8.0, 8.0
    for _ in range(60):
        z = (low + high) / 2
        low, high = (z, high) if 0.5 * math.erfc(z / math.sqrt(2)) > share else (low, z)
    return low


def constant_tables():
    rotary = np.zeros((P, 4 * 512), np.float32)
    inv = (1.0 / np.float32(10000.0) ** (np.arange(0, DH, 2, dtype=np.float32) / DH)).astype(np.float32)
    angle = np.outer(np.arange(S, dtype=np.float32), inv).astype(np.float32)
    cos = np.concatenate([np.cos(angle), np.cos(angle)], -1)
    sin = np.concatenate([-np.sin(angle), np.sin(angle)], -1)

    def rows(a):
        return a.reshape(TILES, P, DH).transpose(1, 0, 2).reshape(P, TILES * DH)
    scale = DH ** -0.5
    rotary[:, R_COSQ:R_COSQ + 512] = rows(cos) * scale
    rotary[:, R_SINQ:R_SINQ + 512] = rows(sin) * scale
    rotary[:, R_COSK:R_COSK + 512] = rows(cos)
    rotary[:, R_SINK:R_SINK + 512] = rows(sin)
    table = np.zeros((P, C_WIDTH), np.float32)
    table[:, C_IDENT:C_IDENT + P] = np.eye(P)
    table[:, C_MASK:C_MASK + P] = np.triu(np.full((P, P), NEG), 1)
    table[:, C_RANK:C_RANK + WINDOW] = np.arange(WINDOW)
    for t in range(TILES):
        table[:, C_INV + t] = 1.0 / ((t + 1) * P)
        for p in range(P):
            valid = t * P + p + 1
            if valid <= TOPK:
                continue
            z = deviate(min(AIM_FIRST / valid, 0.97))
            table[p, C_Z + t] = z
            table[p, C_STEP + t] = 1.0 / (valid * density(z))
            table[p, C_AIM + t] = min(AIM, (valid + TOPK) / 2) - (t + 1) * P / 2
    table[:TOPK, C_OPEN] = BIG
    table[TOPK:, C_SEARCHED] = 1.0
    return table, rotary


def build(nc, x, wqT, wkT, wvT, woT, wrT, wkfT, wvfT, mu_r, mu_k, table, rotary, out):
    ctx = ExitStack()
    with ctx:
        def sb(name, shape, dt=F32):
            return ctx.enter_context(nc.sbuf_tensor(name, shape, dt))

        def sem(name):
            return ctx.enter_context(nc.semaphore(name))

        consts = sb("consts", [P, C_WIDTH])
        ident = consts[:, C_IDENT:C_IDENT + P]
        ident16 = sb("ident16", [P, P], BF16)
        mask16 = sb("mask16", [P, P], BF16)
        ones = sb("ones", [P, 1])
        eps = sb("eps", [P, 1])
        Wo = sb("Wo", [P, PAIRS, D])
        mix = sb("mix", [P, 4])

        QT = sb("QT", [P, PAIRS, S])
        KT = sb("KT", [P, KV, 2, S])
        V = sb("V", [P, TILES, KV, DH + 1])
        resid = sb("resid", [P, TILES, D])
        base = sb("base", [P, TILES, HEADS])
        slope = sb("slope", [P, TILES, HEADS])

        depth = sb("depth", [P, DRING, GROUP, S])
        weight = sb("weight", [P, RING, GROUP, S])
        def room(ring, slot, first=0, size=S):
            return ring[:, slot // GROUP, slot % GROUP, first:first + size]

        def by_tile(a):
            return a.rearrange("p (t c) -> p t c", t=TILES)
        xin = by_tile(room(depth, 0))
        xn = by_tile(room(depth, 1))
        xnT = room(depth, 2)
        Wq = room(depth, 3)
        Wk, Wv = room(depth, 4, 0, 256), room(depth, 4, 256, 256)
        Wr, Wkf, Wvf = [room(depth, 4, 512 + i * P, P) for i in range(3)]
        rot = [room(depth, 5 + i // 2, (i % 2) * 512, 512) for i in range(4)]
        qcos, qsin = room(depth, 7), room(depth, 8)
        qrow = [room(depth, 9), room(depth, 10), room(depth, 11)]
        krow = [room(weight, i, 0, 768).rearrange("p (k c) -> p k c", k=KV) for i in range(2)]
        prod = room(weight, 2)
        kcos, ksin = room(weight, 3, 0, 256), room(weight, 3, 256, 256)
        bn, mv = by_tile(room(weight, 3, 512, 48)), by_tile(room(weight, 3, 560, 16))
        rstd, std = room(weight, 3, 576, 8), room(weight, 3, 584, 8)
        gram = [room(weight, 4 + i, 0, 520).rearrange("p (k c) -> p k c", k=KV) for i in range(2)]
        ssum, ssq, mean = [by_tile(room(weight, 4, 520 + i * P, P)) for i in range(3)]
        var, dev = [by_tile(room(weight, 5, 520 + i * P, P)) for i in range(2)]
        xrT, xkT, relu, kact, gate, gden = [room(weight, 6 + i) for i in range(6)]

        zbuf = sb("zbuf", [P, 2, S])
        junk = sb("junk", [P, 2, S], BF16)
        PT = sb("PT", [P, PTS, BANK])
        heads_out = sb("heads_out", [P, HEADS * DH])
        yout = sb("yout", [P, D])
        attn_out = sb("attn_out", [P, D])
        SR = 4
        rowmax = sb("rowmax", [P, SR, GROUP])
        tau1 = sb("tau1", [P, SR, GROUP])
        tau2 = sb("tau2", [P, SR, GROUP])
        tau3 = sb("tau3", [P, SR, GROUP])
        sign1 = sb("sign1", [P, SR, GROUP])
        sign2 = sb("sign2", [P, SR, GROUP])
        sign3 = sb("sign3", [P, SR, GROUP])
        step_a = sb("step_a", [P, GROUP])
        step_b = sb("step_b", [P, GROUP])
        step_c = sb("step_c", [P, GROUP])
        step_d = sb("step_d", [P, GROUP])
        rank = sb("rank", [P, SR, GROUP])
        outside = sb("outside", [P, SR, GROUP])
        cand = sb("cand", [P, GROUP, SEGMENTS, 8])
        rest = sb("rest", [P, GROUP, SEGMENTS * 8])
        sorted24 = sb("sorted24", [P, GROUP, WINDOW])
        pick = sb("pick", [P, GROUP, WINDOW])
        segmin = sb("segmin", [P, GROUP])
        fail = sb("fail", [P, GROUP + 1])
        fail_b = sb("fail_b", [P, GROUP])
        fail_c = sb("fail_c", [P, GROUP])
        failed = sb("failed", [1, GROUP + 1], I32)
        thr = sb("thr", [P, 2, GROUP])
        best8 = sb("best8", [P, 8])
        outT = sb("outT", [DH + 1, BANK])
        rden = sb("rden", [P, GROUP])
        slow = zbuf[:, 0, :]

        psum = ctx.enter_context(nc.psum_tensor("psum", [P, 8, BANK], F32))

        names = """tables_loaded x_loaded p_stat p_std p_xn p_xnT p_xnT_read p_proj p_proj_read p_rope p_qrow
            p_qT p_kT p_T_read p_gram p_gram_read p_stats p_stats_read p_var p_dev p_pad p_mixed p_ffn p_resid
            p_relu p_exp p_kact p_v dve_step pool_step act_step thr_step
            scores_done scores_read depth_ready exp_ready tau1_ready tau2_ready tau3_ready count1 count2 count3
            fail_ready fail_summed fail_read weight_ready chunk_done chunk_read chunk_used sums_read back_done out_read
            attn_ready y_read stored slow_step rank_ready""".split()
        s = {n: sem(n) for n in names}
        main_loaded = sem("main_loaded")

        with nc.Block() as block:
            @block.sync
            def _(sp):
                loads = ((consts[:], table),
                         (Wo[:], woT.rearrange("(c p) n -> p c n", p=P)),
                         (mix[:, 0:1], mu_r), (mix[:, 1:2], mu_k))
                for dst, src in loads:
                    sp.dma_start(dst, src).then_inc(main_loaded, 16)
                sp.wait_ge(main_loaded, 16 * len(loads))

            @block.vector
            def _(dve):
                dve.memset(ones[:], 1.0)
                dve.memset(eps[:], EPS)
                dve.memset(V[:, :, :, DH:DH + 1], 1.0)
                dve.wait_ge(main_loaded, 64)
                dve.tensor_copy(ident16[:], ident)
                dve.tensor_copy(mask16[:], consts[:, C_MASK:C_MASK + P])
                dve.tensor_scalar(mix[:, 2:4], mix[:, 0:2], -1.0, 1.0, ALU.mult, ALU.add)

        x_rows = x.rearrange("b (t p) c -> b p t c", p=P)
        out_rows = out.rearrange("b (t p) c -> b p t c", p=P)

        with nc.Fori(0, B) as b:
            with nc.Block() as block:
                @block.sync
                def _(sp):
                    sp.dma_start(xin, x_rows[b]).then_inc(s["x_loaded"], 16)
                    for dst, src in ((Wq, wqT), (Wk, wkT), (Wv, wvT), (Wr, wrT), (Wkf, wkfT), (Wvf, wvfT)):
                        sp.dma_start(dst, src).then_inc(s["tables_loaded"], 16)
                    for i in range(4):
                        sp.dma_start(rot[i], rotary[:, i * 512:(i + 1) * 512]).then_inc(s["tables_loaded"], 16)
                    sp.wait_ge(s["tables_loaded"], 160)

                @block.gpsimd
                def _(pool):
                    pool.memset(krow[0], 0.0)
                    pool.memset(krow[1], 0.0).then_inc(s["p_pad"], 1)
                    for t in range(TILES):
                        pool.wait_ge(s["p_rope"], t + 1)
                        if t >= 3:
                            pool.wait_ge(s["p_stats_read"], 4 * (t - 2))
                            pool.wait_ge(s["p_qT"], 2 * (t - 2))
                        pool.tensor_tensor(qrow[t % 3], qcos, qsin, ALU.add).then_inc(s["p_qrow"], 1)

                @block.vector
                def _(dve):
                    n = [0]

                    def link(ins):
                        n[0] += 1
                        ins.then_inc(s["dve_step"], 1)
                        dve.wait_ge(s["dve_step"], n[0])

                    def rotate(t):
                        cos = [r[:, t * DH:(t + 1) * DH] for r in rot]
                        dve.wait_ge(s["p_proj"], t + 1)
                        if t:
                            dve.wait_ge(s["p_qrow"], t)
                        for half in range(2):
                            q = psum[:, half, :].rearrange("p (h d) -> p h d", d=DH)
                            oc = qcos[:, half * BANK:(half + 1) * BANK].rearrange("p (h d) -> p h d", d=DH)
                            os = qsin[:, half * BANK:(half + 1) * BANK].rearrange("p (h d) -> p h d", d=DH)
                            dve.tensor_tensor(oc, q, cos[0].unsqueeze(1).to_broadcast([P, 8, DH]), ALU.mult)
                            dve.tensor_tensor(os[:, :, 0:32], q[:, :, 32:64],
                                              cos[1][:, 0:32].unsqueeze(1).to_broadcast([P, 8, 32]), ALU.mult)
                            last = dve.tensor_tensor(os[:, :, 32:64], q[:, :, 0:32],
                                                     cos[1][:, 32:64].unsqueeze(1).to_broadcast([P, 8, 32]), ALU.mult)
                        last.then_inc(s["p_rope"], 1)
                        k = psum[:, 2, 0:256].rearrange("p (h d) -> p h d", d=DH)
                        kc = kcos.rearrange("p (h d) -> p h d", d=DH)
                        ks = ksin.rearrange("p (h d) -> p h d", d=DH)
                        dve.tensor_tensor(kc, k, cos[2].unsqueeze(1).to_broadcast([P, KV, DH]), ALU.mult)
                        dve.tensor_tensor(ks[:, :, 0:32], k[:, :, 32:64],
                                          cos[3][:, 0:32].unsqueeze(1).to_broadcast([P, KV, 32]), ALU.mult)
                        dve.tensor_tensor(ks[:, :, 32:64], k[:, :, 0:32],
                                          cos[3][:, 32:64].unsqueeze(1).to_broadcast([P, KV, 32]), ALU.mult)
                        link(dve.tensor_copy(V[:, t, :, 0:DH], psum[:, 2, 256:512].rearrange("p (h d) -> p h d", d=DH)))
                        if t >= 2:
                            dve.wait_ge(s["p_gram"], t - 1)
                        dve.tensor_tensor(krow[t % 2][:, :, 64:128], kc, ks, ALU.add).then_inc(s["p_proj_read"], 1)

                    def score_sums(t):
                        for quad in range(4):
                            dve.wait_ge(s["p_stats"], 4 * t + quad + 1)
                            st = psum[:, 6 + quad % 2, 0:260].rearrange("p (h c) -> p h c", h=4)
                            part = slice(quad * 256, (quad + 1) * 256)
                            dve.tensor_tensor(prod[:, part].rearrange("p (h d) -> p h d", h=4), st[:, :, 0:64],
                                              qrow[t % 3][:, part].rearrange("p (h d) -> p h d", h=4), ALU.mult)
                            dve.tensor_copy(ssum[:, t, 4 * quad:4 * quad + 4], st[:, :, 64]).then_inc(s["p_stats_read"], 1)
                        dve.wait_ge(s["p_stats_read"], 4 * t + 4)
                        link(dve.tensor_reduce(ssq[:, t, :], prod.rearrange("p (h d) -> p h d", h=HEADS), AXIS.X, ALU.add))

                    dve.wait_ge(s["x_loaded"], 16)
                    for t in range(TILES):
                        last = dve.bn_stats(bn[:, t, :], xin[:, t, :])
                    link(last)
                    for t in range(TILES):
                        last = dve.bn_aggr(mv[:, t, :], bn[:, t, :])
                    last.then_inc(s["p_stat"], 1)
                    dve.wait_ge(s["p_std"], 1)
                    link(dve.reciprocal(rstd, std))
                    for t in range(TILES):
                        dve.tensor_scalar(xn[:, t, :], xin[:, t, :], mv[:, t, 0:1], rstd[:, t:t + 1],
                                          ALU.subtract, ALU.mult).then_inc(s["p_xn"], 1)
                    dve.wait_ge(s["p_xnT"], TILES // 2)
                    dve.tensor_copy(xnT[:, 0:BANK], psum[:, 0, :]).then_inc(s["p_xnT_read"], 1)
                    dve.wait_ge(s["p_xnT_read"], 2)
                    dve.tensor_scalar(xkT, xnT, mix[:, 1:2], None, ALU.mult)
                    link(dve.tensor_scalar(xrT, xnT, mix[:, 0:1], None, ALU.mult))
                    dve.scalar_tensor_tensor(xkT[:, 1:S], xnT[:, 0:S - 1], mix[:, 3:4], xkT[:, 1:S], ALU.mult, ALU.add)\
                       .then_inc(s["p_mixed"], 1)
                    dve.scalar_tensor_tensor(xrT[:, 1:S], xnT[:, 0:S - 1], mix[:, 2:3], xrT[:, 1:S], ALU.mult, ALU.add)\
                       .then_inc(s["p_mixed"], 1)
                    dve.wait_ge(s["p_pad"], 1)
                    dve.wait_ge(s["tables_loaded"], 160)
                    for r in range(TILES + 2):
                        if r < TILES:
                            rotate(r)
                        if r == 0:
                            dve.wait_ge(s["p_relu"], 2)
                            dve.tensor_tensor(kact, relu, relu, ALU.mult).then_inc(s["p_kact"], 1)
                            dve.wait_ge(s["p_exp"], 2)
                            link(dve.tensor_scalar(gden, gate, 1.0, None, ALU.add))
                            link(dve.reciprocal(gate, gden))
                        if r == 1:
                            dve.wait_ge(s["p_v"], 1)
                            link(dve.tensor_tensor(gden, gate, psum[:, 6:8, :].rearrange("p a c -> p (a c)"), ALU.mult))
                            dve.tensor_tensor(resid[:].rearrange("p t c -> p (t c)"), gden,
                                              xin.rearrange("p t c -> p (t c)"), ALU.add).then_inc(s["p_resid"], 1)
                        if r >= 2:
                            score_sums(r - 2)
                    inv = consts[:, C_INV:C_INV + TILES].unsqueeze(2).to_broadcast([P, TILES, HEADS])
                    dve.tensor_tensor(mean, ssum, inv, ALU.mult)
                    link(dve.tensor_tensor(ssq, ssq, inv, ALU.mult))
                    link(dve.tensor_tensor(var, mean, mean, ALU.mult))
                    link(dve.tensor_tensor(var, ssq, var, ALU.subtract))
                    dve.tensor_scalar(var, var, 0.0, None, ALU.max).then_inc(s["p_var"], 1)
                    dve.wait_ge(s["p_dev"], 1)
                    z = consts[:, C_Z:C_Z + TILES].unsqueeze(2).to_broadcast([P, TILES, HEADS])
                    step = consts[:, C_STEP:C_STEP + TILES].unsqueeze(2).to_broadcast([P, TILES, HEADS])
                    link(dve.tensor_tensor(base[:], dev, z, ALU.mult))
                    dve.tensor_tensor(base[:], base[:], mean, ALU.add)
                    link(dve.tensor_tensor(slope[:], dev, step, ALU.mult))

                @block.scalar
                def _(act):
                    act.wait_ge(s["p_stat"], 1)
                    act.activation(std, mv[:, :, 1], ACT.Sqrt, bias=eps[:, 0:1]).then_inc(s["p_std"], 1)
                    act.wait_ge(s["p_xnT"], TILES)
                    act.activation(xnT[:, BANK:S], psum[:, 1, :], ACT.Copy).then_inc(s["p_xnT_read"], 1)
                    act.wait_ge(s["p_ffn"], 1)
                    for half in range(2):
                        act.activation(relu[:, half * BANK:(half + 1) * BANK], psum[:, 6 + half, :], ACT.Relu)\
                           .then_inc(s["p_relu"], 1)
                    act.wait_ge(s["p_ffn"], 2)
                    for half in range(2):
                        act.activation(gate[:, half * BANK:(half + 1) * BANK], psum[:, 4 + half, :], ACT.Exp, scale=-1.0)\
                           .then_inc(s["p_exp"], 1)
                    for t in range(TILES):
                        for half in range(2):
                            act.wait_ge(s["p_qT"], 2 * t + half + 1)
                            act.activation(QT[:, 4 * half:4 * half + 4, t * P:(t + 1) * P],
                                           psum[:, 3, :].rearrange("p (a c) -> p a c", a=4), ACT.Copy)\
                               .then_inc(s["p_T_read"], 1)
                        for half in range(2):
                            act.wait_ge(s["p_kT"], 2 * t + half + 1)
                            act.activation(KT[:, 2 * half:2 * half + 2, :, t * P:(t + 1) * P],
                                           psum[:, 3, :].rearrange("p (a v c) -> p a v c", a=2, v=2), ACT.Copy)\
                               .then_inc(s["p_T_read"], 1)
                        act.wait_ge(s["p_gram"], t + 1)
                        if t >= 2:
                            act.wait_ge(s["p_stats"], 4 * (t - 1))
                        for half in range(2):
                            act.activation(gram[t % 2][:, 2 * half:2 * half + 2, :],
                                           psum[:, 4 + half, 0:260].rearrange("p (k c) -> p k c", k=2), ACT.Copy)\
                               .then_inc(s["p_gram_read"], 1)
                    act.wait_ge(s["p_var"], 1)
                    act.activation(dev, var, ACT.Sqrt).then_inc(s["p_dev"], 1)

                @block.tensor
                def _(pe):
                    def projections(t):
                        xt = xnT[:, t * P:(t + 1) * P]
                        if t:
                            pe.wait_ge(s["p_proj_read"], t)
                        pe.matmul(psum[:, 0, :], xt, Wq[:, 0:BANK], start=True, stop=True)
                        pe.matmul(psum[:, 1, :], xt, Wq[:, BANK:2 * BANK], start=True, stop=True)
                        pe.matmul(psum[:, 2, 0:256], xt, Wk, start=True, stop=True)
                        pe.matmul(psum[:, 2, 256:512], xt, Wv, start=True, stop=True).then_inc(s["p_proj"], 1)

                    def mix_first():
                        pe.wait_ge(s["p_mixed"], 1)
                        for half in range(2):
                            last = pe.matmul(psum[:, 6 + half, :], Wkf, xkT[:, half * BANK:(half + 1) * BANK],
                                             start=True, stop=True)
                        last.then_inc(s["p_ffn"], 1)
                        pe.wait_ge(s["p_mixed"], 2)
                        for t in range(TILES):
                            last = pe.matmul(psum[:, 4 + t // 4, (t % 4) * P:(t % 4 + 1) * P], xrT[:, t * P:(t + 1) * P], Wr,
                                             start=True, stop=True)
                        last.then_inc(s["p_ffn"], 1)

                    def mix_second():
                        pe.wait_ge(s["p_relu"], 2)
                        pe.wait_ge(s["p_kact"], 1)
                        for t in range(TILES):
                            last = pe.matmul(psum[:, 6 + t // 4, (t % 4) * P:(t % 4 + 1) * P], kact[:, t * P:(t + 1) * P], Wvf,
                                             start=True, stop=True)
                        last.then_inc(s["p_v"], 1)

                    def turn(t, c):
                        if 4 * t + c:
                            pe.wait_ge(s["p_T_read"], 4 * t + c)
                        if c == 0:
                            pe.wait_ge(s["p_qrow"], t + 1)
                        if c == 2:
                            pe.wait_ge(s["p_proj_read"], t + 1)
                        for a in range(4):
                            if c < 2:
                                rows = qrow[t % 3][:, (4 * c + a) * P:(4 * c + a + 1) * P]
                            else:
                                kv, first = 2 * (c - 2) + a // 2, 64 * (1 - a % 2)
                                rows = krow[t % 2][:, kv, first:first + P]
                            last = pe.transpose(psum[:, 3, a * P:(a + 1) * P], rows, ident)
                        last.then_inc(s["p_qT"] if c < 2 else s["p_kT"], 1)

                    def key_sums(t):
                        if t:
                            pe.wait_ge(s["p_gram_read"], 2 * t)
                        else:
                            pe.wait_ge(s["p_exp"], 2)
                        for kv in range(KV):
                            g = psum[:, 4 + kv // 2, (kv % 2) * 130:(kv % 2) * 130 + 130]
                            for v in range(2):
                                lhs = krow[t % 2][:, kv, 64 * (1 - v):64 * (1 - v) + P]
                                pe.matmul(g[:, 65 * v:65 * v + 64], lhs, krow[t % 2][:, kv, 64:128],
                                          start=(t == 0), stop=True, skip_group_check=True)
                                last = pe.matmul(g[:, 65 * v + 64:65 * v + 65], lhs, ones[:],
                                                 start=(t == 0), stop=True, skip_group_check=True)
                        last.then_inc(s["p_gram"], 1)

                    def row_sums(t, quad):
                        i = 4 * t + quad
                        if i >= 2:
                            pe.wait_ge(s["p_stats_read"], i - 1)
                        else:
                            pe.wait_ge(s["p_resid"], 1)
                        if quad == 0:
                            pe.wait_ge(s["p_gram_read"], 2 * t + 2)
                        for a in range(2):
                            last = pe.matmul(psum[:, 6 + quad % 2, 130 * a:130 * a + 130],
                                             QT[:, 2 * quad + a, t * P:(t + 1) * P], gram[t % 2][:, quad, :],
                                             start=True, stop=True)
                        last.then_inc(s["p_stats"], 1)

                    for t in range(TILES):
                        pe.wait_ge(s["p_xn"], t + 1)
                        pe.transpose(psum[:, t // 4, (t % 4) * P:(t % 4 + 1) * P], xn[:, t, :], ident)\
                          .then_inc(s["p_xnT"], 1)
                    pe.wait_ge(s["p_xnT_read"], 2)
                    pe.wait_ge(s["tables_loaded"], 160)
                    for r in range(TILES + 2):
                        if r < TILES:
                            projections(r)
                        if r == 0:
                            mix_first()
                        if r == 1:
                            mix_second()
                        for c in range(4):
                            if 1 <= r <= TILES:
                                turn(r - 1, c)
                            if r >= 2:
                                row_sums(r - 2, c)
                        if 1 <= r <= TILES:
                            key_sums(r - 1)

            def key_tiles(k):
                return GROUPS[k][0] + 1

            def live(k):
                return 0 <= k < NG

            def ends_tile(k):
                return live(k) and GROUPS[k][1] == KV - 1

            bank, kept, uses, banks, rooms = {}, {}, [], 0, 0
            for rnd in range(NG + 5):
                if live(rnd - 2):
                    bank["weights", rnd - 2], kept["weights", rnd - 2] = banks, rooms
                    banks, rooms = banks + key_tiles(rnd - 2), rooms + key_tiles(rnd - 2)
                    uses += [(uses[-1] if uses else 0) + 1 + i for i in range(key_tiles(rnd - 2))]
                if ends_tile(rnd - 4):
                    bank["heads", rnd - 4], kept["heads", rnd - 4] = banks, rooms
                    banks, rooms = banks + 3, rooms + 2
                    uses += [(uses[-1] if uses else 0) + 1] * 2

            with nc.Block() as block:
                @block.tensor
                def _(pe):
                    def scores(k, j):
                        t, kv = GROUPS[k]
                        u, h, L = GROUP * k + j, GROUP * kv + j, (t + 1) * P
                        if u >= 2:
                            pe.wait_ge(s["scores_read"], u - 1)
                        for c in range(0, L, BANK):
                            w = min(BANK, L - c)
                            bank = psum[:, 2 * (u % 2) + c // BANK, :]
                            diagonal = c + w == L
                            pe.matmul(bank[:, 0:w], QT[:, h // 2, t * P:(t + 1) * P], KT[:, kv, h % 2, c:c + w],
                                      start=True, stop=not diagonal)
                            if diagonal:
                                pe.matmul(bank[:, w - P:w], ident16[:], mask16[:], start=False, stop=True)\
                                  .then_inc(s["scores_done"], 1)

                    def transposes(k, i):
                        q = bank["weights", k] + i
                        if q >= 2:
                            pe.wait_ge(s["chunk_read"], q - 1)
                        for j in range(GROUP):
                            if i == 0:
                                pe.wait_ge(s["weight_ready"], GROUP * k + j + 1)
                            last = pe.transpose(psum[:, 4 + q % 2, j * P:(j + 1) * P],
                                                weight[:, k % RING, j, i * P:(i + 1) * P], ident)
                        last.then_inc(s["chunk_done"], 1)

                    def products(k, i):
                        t, kv = GROUPS[k]
                        pe.wait_ge(s["chunk_read"], bank["weights", k] + i + 1)
                        if i == 0 and k:
                            pe.wait_ge(s["sums_read"], k)
                        pe.matmul(psum[0:DH + 1, 6, :], V[:, i, kv, :], PT[:, (kept["weights", k] + i) % PTS, :],
                                  start=(i == 0), stop=(i == t)).then_inc(s["chunk_used"], 1)

                    def back(k):
                        pe.wait_ge(s["sums_read"], k + 1)
                        pe.wait_ge(s["out_read"], k)
                        pe.wait_ge(s["fail_read"], min(k + 2, NG))
                        for j in range(GROUP):
                            last = pe.transpose(psum[:, 7, j * (DH + 1):(j + 1) * (DH + 1)], outT[:, j * P:(j + 1) * P],
                                                ident[0:DH + 1, 0:DH + 1])
                        last.then_inc(s["back_done"], 1)

                    def sum_fails(k):
                        pe.wait_ge(s["fail_ready"], k + 1)
                        if k >= 3:
                            pe.wait_ge(s["out_read"], k - 2)
                        if k:
                            pe.wait_ge(s["fail_read"], k)
                        pe.matmul(psum[0:1, 7, 320:320 + GROUP + 1], ones[:], fail[:], start=True, stop=True)\
                          .then_inc(s["fail_summed"], 1)

                    def project(k):
                        q = bank["heads", k]
                        pe.wait_ge(s["out_read"], k + 1)
                        for i in range(2):
                            pe.wait_ge(s["chunk_read"], q + i - 1)
                            for a in range(4):
                                last = pe.transpose(psum[:, 4 + (q + i) % 2, a * P:(a + 1) * P],
                                                    heads_out[:, (4 * i + a) * P:(4 * i + a + 1) * P], ident)
                            last.then_inc(s["chunk_done"], 1)
                        for i in range(2):
                            pe.wait_ge(s["chunk_read"], q + i + 1)
                            for a in range(4):
                                last = pe.matmul(psum[:, 4 + q % 2, 0:D], PT[:, (kept["heads", k] + i) % PTS, a * P:(a + 1) * P],
                                                 Wo[:, 4 * i + a, :], start=(i + a == 0), stop=(i + a == 4))
                            last.then_inc(s["chunk_used"] if i == 0 else s["chunk_done"], 1)

                    for j in range(GROUP):
                        scores(0, j)
                    for j in range(2):
                        scores(1, j)
                    for rnd in range(NG + 5):
                        k = rnd - 2
                        if live(k):
                            transposes(k, 0)
                            for i in range(key_tiles(k)):
                                if i + 1 < key_tiles(k):
                                    transposes(k, i + 1)
                                products(k, i)
                        if live(rnd - 3):
                            back(rnd - 3)
                        if live(rnd - 1):
                            sum_fails(rnd - 1)
                        for k, j in ((rnd + 1, 2), (rnd + 1, 3), (rnd + 2, 0), (rnd + 2, 1)):
                            if live(k):
                                scores(k, j)
                        if ends_tile(rnd - 4):
                            project(rnd - 4)

                @block.scalar
                def _(act):
                    n = [0]

                    def signs(k, tau, acc, counted, between):
                        L = key_tiles(k) * P
                        for j in range(GROUP):
                            if n[0] >= 2:
                                act.wait_ge(s["act_step"], n[0] - 1)
                            act.activation(junk[:, n[0] % 2, 0:L], depth[:, k % DRING, j, 0:L], ACT.Sign,
                                           bias=tau[:, k % SR, j:j + 1], scale=-1.0, accum_out=acc[:, k % SR, j:j + 1])\
                               .then_inc(s["act_step"], 1)
                            n[0] += 1
                            between(j)
                        act.wait_ge(s["act_step"], n[0])
                        act.activation(acc[:, k % SR, :], acc[:, k % SR, :], ACT.Copy).then_inc(counted, 1)

                    def keep(q, m):
                        act.wait_ge(s["chunk_done"], q + 1)
                        if m >= PTS:
                            act.wait_ge(s["chunk_used"], uses[m - PTS])
                        act.activation(PT[:, m % PTS, :], psum[:, 4 + q % 2, :], ACT.Copy).then_inc(s["chunk_read"], 1)

                    for rnd in range(NG + 6):
                        k = rnd - 5
                        if ends_tile(k):
                            act.wait_ge(s["chunk_done"], bank["heads", k] + 3)
                            if k >= KV:
                                act.wait_ge(s["y_read"], k // KV)
                            act.activation(attn_out[:], psum[:, 4 + bank["heads", k] % 2, 0:D], ACT.Copy)\
                               .then_inc(s["chunk_read"], 1)
                        k = rnd - 3
                        if live(k):
                            act.wait_ge(s["chunk_used"], uses[kept["weights", k] + key_tiles(k) - 1])
                            if k:
                                act.wait_ge(s["back_done"], k)
                            act.activation(outT[:], psum[0:DH + 1, 6, :], ACT.Copy).then_inc(s["sums_read"], 1)
                        k = rnd - 2
                        todo = [(bank["weights", k] + i, kept["weights", k] + i) for i in range(key_tiles(k))] if live(k) else []

                        def chunks_left(left):
                            while len(todo) > max(left, 0):
                                keep(*todo.pop(0))
                        k = rnd
                        if live(k):
                            L = key_tiles(k) * P
                            act.wait_ge(s["tau1_ready"], k + 1)
                            signs(k, tau1, sign1, s["count1"], lambda j: chunks_left(7 - j // 2))
                            if k >= RING:
                                act.wait_ge(s["chunk_done"], bank["weights", k - RING] + key_tiles(k - RING))
                            for j in range(GROUP):
                                act.activation(weight[:, k % RING, j, 0:L], depth[:, k % DRING, j, 0:L], ACT.Exp, scale=-1.0)\
                                   .then_inc(s["exp_ready"], 1)
                                chunks_left(5 - j)
                            act.wait_ge(s["tau2_ready"], k + 1)
                            signs(k, tau2, sign2, s["count2"], lambda j: chunks_left(1 - j))
                            act.wait_ge(s["tau3_ready"], k + 1)
                            signs(k, tau3, sign3, s["count3"], lambda j: None)
                        chunks_left(0)
                        k = rnd - 4
                        if ends_tile(k):
                            for i in range(2):
                                keep(bank["heads", k] + i, kept["heads", k] + i)

                @block.gpsimd
                def _(pool):
                    n = [0]

                    def link(ins):
                        n[0] += 1
                        ins.then_inc(s["pool_step"], 1)
                        pool.wait_ge(s["pool_step"], n[0])

                    def missing(k, acc):
                        t, kv = GROUPS[k]
                        link(pool.tensor_scalar(step_a[:], acc[:, k % SR, :], -0.5, consts[:, C_AIM + t:C_AIM + t + 1],
                                                ALU.mult, ALU.add))
                        link(pool.tensor_tensor(step_b[:], step_a[:], slope[:, t, GROUP * kv:GROUP * (kv + 1)], ALU.mult))

                    def second(k):
                        pool.wait_ge(s["count1"], k + 1)
                        missing(k, sign1)
                        pool.tensor_tensor(tau2[:, k % SR, :], tau1[:, k % SR, :], step_b[:], ALU.add)\
                            .then_inc(s["tau2_ready"], 1)

                    def third(k):
                        t, kv = GROUPS[k]
                        L = (t + 1) * P
                        pool.wait_ge(s["count2"], k + 1)
                        pool.wait_ge(s["tau2_ready"], k + 1)
                        missing(k, sign2)
                        link(pool.tensor_scalar(step_c[:], sign2[:, k % SR, :], float(2 * TOPK - L), None, ALU.is_lt))
                        link(pool.tensor_scalar(step_d[:], sign2[:, k % SR, :], float(2 * (TOPK + WINDOW) - L), None, ALU.is_ge))
                        link(pool.tensor_tensor(step_c[:], step_c[:], step_d[:], ALU.add))
                        link(pool.tensor_tensor(step_b[:], step_b[:], step_c[:], ALU.mult))
                        pool.tensor_tensor(tau3[:, k % SR, :], tau2[:, k % SR, :], step_b[:], ALU.add)\
                            .then_inc(s["tau3_ready"], 1)

                    def ranks(k):
                        L = (GROUPS[k][0] + 1) * P
                        pool.wait_ge(s["count3"], k + 1)
                        pool.wait_ge(s["tau3_ready"], k + 1)
                        link(pool.tensor_scalar(rank[:, k % SR, :], sign3[:, k % SR, :], 0.5, float(L / 2 - TOPK),
                                                ALU.mult, ALU.add))
                        link(pool.tensor_scalar(step_c[:], rank[:, k % SR, :], 0.0, None, ALU.is_lt))
                        link(pool.tensor_scalar(step_d[:], rank[:, k % SR, :], float(WINDOW - 1), None, ALU.is_gt))
                        pool.tensor_tensor(outside[:, k % SR, :], step_c[:], step_d[:], ALU.add).then_inc(s["rank_ready"], 1)

                    def depths(k):
                        t, kv = GROUPS[k]
                        L = (t + 1) * P
                        for j in range(GROUP):
                            pool.wait_ge(s["scores_read"], GROUP * k + j + 1)
                            d = depth[:, k % DRING, j, 0:L]
                            pool.tensor_scalar(d, d, -1.0, rowmax[:, k % SR, j:j + 1], ALU.mult, ALU.add)\
                                .then_inc(s["depth_ready"], 1)
                        pool.tensor_tensor(tau1[:, k % SR, :], rowmax[:, k % SR, :], base[:, t, GROUP * kv:GROUP * (kv + 1)],
                                           ALU.subtract).then_inc(s["tau1_ready"], 1)

                    def finish(k):
                        pool.wait_ge(s["chunk_read"], bank["heads", k] + 3)
                        if k >= KV:
                            pool.wait_ge(s["stored"], 16 * (k // KV))
                        pool.tensor_tensor(yout[:], attn_out[:], resid[:, GROUPS[k][0], :], ALU.add).then_inc(s["y_read"], 1)

                    for rnd in range(NG + 6):
                        if ends_tile(rnd - 5):
                            finish(rnd - 5)
                        if live(rnd):
                            depths(rnd)
                            second(rnd)
                            third(rnd)
                            ranks(rnd)

                @block.vector
                def _(dve):
                    n = [0]

                    def link(ins):
                        n[0] += 1
                        ins.then_inc(s["thr_step"], 1)
                        dve.wait_ge(s["thr_step"], n[0])

                    def mark(ins):
                        n[0] += 1
                        ins.then_inc(s["thr_step"], 1)
                        return n[0]

                    def take_scores(k, heads):
                        L = key_tiles(k) * P
                        for j in heads:
                            u = GROUP * k + j
                            dve.wait_ge(s["scores_done"], u + 1)
                            if k >= DRING:
                                dve.wait_ge(s["weight_ready"], GROUP * (k - DRING) + j + 1)
                            dve.tensor_scalar(depth[:, k % DRING, j, 0:L],
                                              psum[:, 2 * (u % 2):2 * (u % 2) + 2, :].rearrange("p a c -> p (a c)")[:, 0:L],
                                              1.0, None, ALU.mult, ALU.max, accum_out=rowmax[:, k % SR, j:j + 1])\
                               .then_inc(s["scores_read"], 1)

                    def thresholds(k):
                        t, kv = GROUPS[k]
                        L = (t + 1) * P
                        w = L // SEGMENTS
                        heads = range(GROUP)
                        dve.wait_ge(s["rank_ready"], k + 1)

                        def select(j):
                            d = depth[:, k % DRING, j, 0:L]
                            return mark(dve.scalar_tensor_tensor(zbuf[:, j % 2, 0:L], d, tau3[:, k % SR, j:j + 1], d,
                                                                 ALU.is_le, ALU.mult))
                        selected, found = {0: select(0), 1: select(1)}, {}
                        for j in heads:
                            dve.wait_ge(s["thr_step"], selected[j])
                            for g in range(SEGMENTS):
                                last = dve.max(cand[:, j, g, :], zbuf[:, j % 2, g * w:(g + 1) * w])
                            found[j] = mark(last)
                            if 1 <= j < 3:
                                dve.wait_ge(s["thr_step"], found[j - 1])
                                selected[j + 1] = select(j + 1)
                        flat = [cand[:, j, :, :].rearrange("p a c -> p (a c)") for j in heads]
                        source, done = flat, [found[j] for j in heads]
                        for lot in range(WINDOW // 8):
                            for j in heads:
                                dve.wait_ge(s["thr_step"], done[j])
                                done[j] = mark(dve.max(sorted24[:, j, 8 * lot:8 * lot + 8], source[j]))
                            if lot + 1 < WINDOW // 8:
                                for j in heads:
                                    dve.wait_ge(s["thr_step"], done[j])
                                    done[j] = mark(dve.match_replace(rest[:, j, :], sorted24[:, j, 8 * lot:8 * lot + 8],
                                                                     source[j], -1.0))
                                source = [rest[:, j, :] for j in heads]
                        for j in heads:
                            dve.wait_ge(s["thr_step"], done[j])
                            done[j] = mark(dve.scalar_tensor_tensor(pick[:, j, :], consts[:, C_RANK:C_RANK + WINDOW],
                                                                    rank[:, k % SR, j:j + 1], sorted24[:, j, :],
                                                                    ALU.is_equal, ALU.mult, accum_out=thr[:, k % 2, j:j + 1]))
                        if k:
                            dve.wait_ge(s["fail_summed"], k)
                        link(dve.tensor_reduce(segmin[:], cand[:, :, :, 7], AXIS.X, ALU.max))
                        mark(dve.tensor_tensor(fail_c[:], sorted24[:, :, 0], tau3[:, k % SR, :], ALU.is_equal))
                        link(dve.tensor_tensor(fail_b[:], segmin[:], thr[:, k % 2, :], ALU.is_gt))
                        link(dve.tensor_tensor(fail_b[:], fail_b[:], outside[:, k % SR, :], ALU.add))
                        link(dve.tensor_tensor(fail[:, 0:GROUP], fail_c[:], fail_b[:], ALU.add))
                        if t == 0:
                            link(dve.tensor_scalar(fail[:, 0:GROUP], fail[:, 0:GROUP], consts[:, C_SEARCHED:C_SEARCHED + 1],
                                                   None, ALU.mult))
                            link(dve.tensor_scalar(thr[:, k % 2, :], thr[:, k % 2, :], consts[:, C_OPEN:C_OPEN + 1],
                                                   None, ALU.max))
                        dve.tensor_reduce(fail[:, GROUP:GROUP + 1], fail[:, 0:GROUP], AXIS.X, ALU.add)\
                           .then_inc(s["fail_ready"], 1)

                    def exact_head(k, j):
                        t, kv = GROUPS[k]
                        L = (t + 1) * P
                        m = [0]
                        dve.sem_clear(s["slow_step"])

                        def then(ins):
                            m[0] += 1
                            ins.then_inc(s["slow_step"], 1)
                            dve.wait_ge(s["slow_step"], m[0])
                        then(dve.tensor_scalar(slow[:, 0:L], depth[:, k % DRING, j, 0:L], -1.0, None, ALU.mult))
                        for i in range(TOPK // 8):
                            then(dve.max(best8[:], slow[:, 0:L]))
                            if i + 1 < TOPK // 8:
                                then(dve.match_replace(slow[:, 0:L], best8[:], slow[:, 0:L], -BIG))
                        found = thr[:, k % 2, j:j + 1]
                        then(dve.tensor_scalar(found, best8[:, 7:8], -1.0, None, ALU.mult))
                        if t == 0:
                            then(dve.tensor_scalar(found, found, consts[:, C_OPEN:C_OPEN + 1], None, ALU.max))

                    def take_failures(k):
                        dve.wait_ge(s["fail_summed"], k + 1)
                        dve.tensor_copy(failed[:], psum[0:1, 7, 320:320 + GROUP + 1]).then_inc(s["fail_read"], 1)

                    def failures(column):
                        return dve.value_load(failed[0:1, column:column + 1], min_val=0, max_val=GROUP * P * GROUP)

                    def exact(k):
                        dve.wait_ge(s["fail_read"], k + 1)
                        with dve.If(failures(GROUP) > 0):
                            for j in range(GROUP):
                                with dve.If(failures(j) > 0):
                                    exact_head(k, j)

                    def weights(k):
                        L = key_tiles(k) * P
                        dve.wait_ge(s["exp_ready"], GROUP * (k + 1))
                        for j in range(GROUP):
                            e = weight[:, k % RING, j, 0:L]
                            dve.scalar_tensor_tensor(e, depth[:, k % DRING, j, 0:L], thr[:, k % 2, j:j + 1], e,
                                                     ALU.is_le, ALU.mult).then_inc(s["weight_ready"], 1)

                    def normalise(k):
                        t, kv = GROUPS[k]
                        dve.wait_ge(s["back_done"], k + 1)
                        sums = psum[:, 7, 0:GROUP * (DH + 1)].rearrange("p (h d) -> p h d", d=DH + 1)
                        link(dve.reciprocal(rden[:], sums[:, :, DH]))
                        if kv == 0 and k:
                            dve.wait_ge(s["chunk_done"], bank["heads", k - 1] + 2)
                        dve.tensor_tensor(heads_out[:, kv * 256:(kv + 1) * 256].rearrange("p (h d) -> p h d", d=DH),
                                          sums[:, :, 0:DH], rden[:].unsqueeze(2).to_broadcast([P, GROUP, DH]), ALU.mult)\
                           .then_inc(s["out_read"], 1)

                    take_scores(0, range(GROUP))
                    for rnd in range(NG + 5):
                        if live(rnd - 4):
                            normalise(rnd - 4)
                        if live(rnd - 1):
                            thresholds(rnd - 1)
                        if live(rnd + 1):
                            take_scores(rnd + 1, (0,))
                        if live(rnd - 1):
                            take_failures(rnd - 1)
                        if live(rnd + 1):
                            take_scores(rnd + 1, (1,))
                        if live(rnd - 1):
                            exact(rnd - 1)
                            weights(rnd - 1)
                        if live(rnd + 1):
                            take_scores(rnd + 1, (2, 3))

                @block.sync
                def _(sp):
                    for i, t in enumerate(ORDER):
                        sp.wait_ge(s["y_read"], i + 1)
                        sp.dma_start(out_rows[b, :, t, :], yout[:]).then_inc(s["stored"], 16)
                    sp.wait_ge(s["stored"], 16 * TILES)

            with nc.Block() as block:
                @block.sync
                def _(sp):
                    for one in s.values():
                        sp.sem_clear(one)


def kernel(**inputs):
    import concourse.bacc as bacc
    from concourse.bass_utils import run_bass_kernel_spmd
    a = {n.split("L0_")[1]: np.asarray(v) for n, v in inputs.items()}
    arrays = {
        "x": a["attn_x"], "wqT": a["attn_Wq"].T, "wkT": a["attn_Wk"].T, "wvT": a["attn_Wv"].T, "woT": a["attn_Wo"].T,
        "wrT": a["ffn_W_r"].T, "wkfT": a["ffn_W_k"].T, "wvfT": a["ffn_W_v"].T,
        "mu_r": a["ffn_mu_r"].reshape(P, 1), "mu_k": a["ffn_mu_k"].reshape(P, 1), 
    }
    arrays["table"], arrays["rotary"] = constant_tables()
    arrays = {n: np.ascontiguousarray(v) for n, v in arrays.items()}
    nc = bacc.Bacc("TRN2", target_bir_lowering=False, num_devices=1)
    args = {n: nc.dram_tensor(n, v.shape, F32, kind="ExternalInput").ap() for n, v in arrays.items()}
    out = nc.dram_tensor("out", (B, S, D), F32, kind="ExternalOutput").ap()
    build(nc, out=out, **args)
    return run_bass_kernel_spmd(nc, [arrays], core_ids=[0]).results[0]["out"]
```
